# Optimizing a Trainium2 kernel written in Bass

```python
import numpy as np
import jax
import jax.numpy as jnp

def _softmax(x, axis=-1):
    return jax.nn.softmax(x, axis=axis)

def _gelu(x):
    return jax.nn.gelu(x, approximate=True)

def _silu(x):
    return jax.nn.silu(x)

def _sigmoid(x):
    return jax.nn.sigmoid(x)

def _layernorm(x, axis=-1, eps=1e-05):
    m = jnp.mean(x, axis=axis, keepdims=True)
    v = jnp.var(x, axis=axis, keepdims=True)
    return (x - m) / jnp.sqrt(v + eps)

def _scatter_add(tgt, idx, src, axis=0):
    return tgt.at[idx].add(src)

def _segment_sum(src, seg, n):
    return jax.ops.segment_sum(src, seg, n)
kernel_name = 'mk_sandwich_d1_jaxref_r8_23d509'

def setup_inputs(seed: int=0):
    np.random.seed(seed)
    _w = jnp.asarray

    def _L0_attn_setup():
        import jax, jax.numpy as jnp
        import numpy as np
        from jax.lax import associative_scan
        B, S, D, F, G = (4, 512, 128, 512, 32)
        EPS = 1e-06

        def _gate_loop(k, v, q, a):
            kv = (k * v).astype(jnp.complex64)

            def op(e1, e2):
                a1, x1 = e1
                a2, x2 = e2
                return (a1 * a2, a2 * x1 + x2)
            _, h = associative_scan(op, (a, kv), axis=1)
            return q.astype(jnp.complex64) * h

        def _layernorm(x, scale, bias):
            mu = jnp.mean(x, axis=-1, keepdims=True)
            var = jnp.mean(jnp.square(x - mu), axis=-1, keepdims=True)
            return (x - mu) * jax.lax.rsqrt(var + EPS) * scale + bias

        def _groupnorm_complex(y, scale, bias):
            b, s, d = y.shape
            yr = y.reshape(b, s, G, d // G)
            mean = jnp.mean(yr, axis=(1, 3), keepdims=True)
            mean2 = jnp.mean(yr.real ** 2 + yr.imag ** 2, axis=(1, 3), keepdims=True)
            var = mean2 - (mean.real ** 2 + mean.imag ** 2)
            yn = (yr - mean) * jax.lax.rsqrt(var + EPS)
            return yn.reshape(b, s, d) * scale + bias
        key = jax.random.key(seed)
        ks = jax.random.split(key, 16)
        xn = lambda k, shp: jax.random.normal(k, shp, jnp.float32) / np.sqrt(shp[0])
        return {'x': jax.random.normal(ks[0], (B, S, D), jnp.float32), 'Wq': xn(ks[1], (D, D)), 'Wk': xn(ks[2], (D, D)), 'Wv': xn(ks[3], (D, D)), 'Wa': xn(ks[4], (D, 2 * D)), 'Wg': xn(ks[5], (D, D)), 'Wo': xn(ks[6], (D, D)), 'gn_scale': jnp.ones((D,), jnp.float32), 'gn_bias': jnp.zeros((D,), jnp.float32), 'ln1_scale': jnp.ones((D,), jnp.float32), 'ln1_bias': jnp.zeros((D,), jnp.float32), 'W1': xn(ks[7], (D, F)), 'b1': jax.random.normal(ks[8], (F,), jnp.float32) * 1e-06, 'W2': xn(ks[9], (F, D)), 'b2': jax.random.normal(ks[10], (D,), jnp.float32) * 1e-06, 'ln2_scale': jnp.ones((D,), jnp.float32), 'ln2_bias': jnp.zeros((D,), jnp.float32)}
    _L0_attn_in = _L0_attn_setup()

    def _L0_ffn_setup():
        import jax, jax.numpy as jnp
        import numpy as np
        TOP_K = 2
        EPS = 1e-10
        key = jax.random.key(seed)
        k1, k2, k3, k4 = jax.random.split(key, 4)
        B, S, H, E = (4, 256, 128, 8)
        tokens = jax.random.normal(k1, (B, S, H), dtype=jnp.float32)
        router_w = jax.random.normal(k2, (E, H), dtype=jnp.float32) * (1.0 / np.sqrt(H))
        router_b = jax.random.normal(k3, (E,), dtype=jnp.float32) * 0.01
        expert_weights = jax.random.normal(k4, (E, H, H), dtype=jnp.float32) * (1.0 / np.sqrt(H))
        return {'tokens': tokens, 'router_w': router_w, 'router_b': router_b, 'expert_weights': expert_weights}
    _L0_ffn_in = _L0_ffn_setup()
    _d = {'L0_attn_x': _L0_attn_in['x'], 'L0_attn_Wq': _L0_attn_in['Wq'], 'L0_attn_Wk': _L0_attn_in['Wk'], 'L0_attn_Wv': _L0_attn_in['Wv'], 'L0_attn_Wa': _L0_attn_in['Wa'], 'L0_attn_Wg': _L0_attn_in['Wg'], 'L0_attn_Wo': _L0_attn_in['Wo'], 'L0_attn_gn_scale': _L0_attn_in['gn_scale'], 'L0_attn_gn_bias': _L0_attn_in['gn_bias'], 'L0_attn_ln1_scale': _L0_attn_in['ln1_scale'], 'L0_attn_ln1_bias': _L0_attn_in['ln1_bias'], 'L0_attn_W1': _L0_attn_in['W1'], 'L0_attn_b1': _L0_attn_in['b1'], 'L0_attn_W2': _L0_attn_in['W2'], 'L0_attn_b2': _L0_attn_in['b2'], 'L0_attn_ln2_scale': _L0_attn_in['ln2_scale'], 'L0_attn_ln2_bias': _L0_attn_in['ln2_bias'], 'L0_ffn_router_w': _L0_ffn_in['router_w'], 'L0_ffn_router_b': _L0_ffn_in['router_b'], 'L0_ffn_expert_weights': _L0_ffn_in['expert_weights']}
    _x0 = _d['L0_attn_x']
    _d['L0_attn_x'] = jax.random.normal(jax.random.fold_in(jax.random.key(seed), 1), (8, 256, 128), dtype=_x0.dtype)
    del _x0
    return _d

def reference(L0_attn_x, L0_attn_Wq, L0_attn_Wk, L0_attn_Wv, L0_attn_Wa, L0_attn_Wg, L0_attn_Wo, L0_attn_gn_scale, L0_attn_gn_bias, L0_attn_ln1_scale, L0_attn_ln1_bias, L0_attn_W1, L0_attn_b1, L0_attn_W2, L0_attn_b2, L0_attn_ln2_scale, L0_attn_ln2_bias, L0_ffn_router_w, L0_ffn_router_b, L0_ffn_expert_weights):

    def _L0_attn_ref(x, Wq, Wk, Wv, Wa, Wg, Wo, gn_scale, gn_bias, ln1_scale, ln1_bias, W1, b1, W2, b2, ln2_scale, ln2_bias):
        import jax, jax.numpy as jnp
        import numpy as np
        from jax.lax import associative_scan
        B, S, D, F, G = (4, 512, 128, 512, 32)
        EPS = 1e-06

        def _gate_loop(k, v, q, a):
            kv = (k * v).astype(jnp.complex64)

            def op(e1, e2):
                a1, x1 = e1
                a2, x2 = e2
                return (a1 * a2, a2 * x1 + x2)
            _, h = associative_scan(op, (a, kv), axis=1)
            return q.astype(jnp.complex64) * h

        def _layernorm(x, scale, bias):
            mu = jnp.mean(x, axis=-1, keepdims=True)
            var = jnp.mean(jnp.square(x - mu), axis=-1, keepdims=True)
            return (x - mu) * jax.lax.rsqrt(var + EPS) * scale + bias

        def _groupnorm_complex(y, scale, bias):
            b, s, d = y.shape
            yr = y.reshape(b, s, G, d // G)
            mean = jnp.mean(yr, axis=(1, 3), keepdims=True)
            mean2 = jnp.mean(yr.real ** 2 + yr.imag ** 2, axis=(1, 3), keepdims=True)
            var = mean2 - (mean.real ** 2 + mean.imag ** 2)
            yn = (yr - mean) * jax.lax.rsqrt(var + EPS)
            return yn.reshape(b, s, d) * scale + bias
        q = x @ Wq
        k = x @ Wk
        v = x @ Wv
        a = x @ Wa
        a_real, a_imag = jnp.split(a, 2, axis=-1)
        a_c = a_real + 1j * a_imag
        mag = jnp.abs(a_c)
        phase = jnp.angle(a_c)
        a_c = jax.nn.sigmoid(mag) * jnp.exp(1j * phase)
        g = (x @ Wg).astype(jnp.complex64)
        y = _gate_loop(k, v, q, a_c)
        y = _groupnorm_complex(y, gn_scale, gn_bias)
        silu_g = g / (1.0 + jnp.exp(-g))
        y = y * silu_g
        y = (y @ Wo.astype(jnp.complex64)).real
        x = _layernorm(x + y, ln1_scale, ln1_bias)
        h = jax.nn.gelu(x @ W1 + b1)
        out = x + (h @ W2 + b2)
        return _layernorm(out, ln2_scale, ln2_bias)

    def _L0_ffn_ref(tokens, router_w, router_b, expert_weights):
        import jax, jax.numpy as jnp
        import numpy as np
        TOP_K = 2
        EPS = 1e-10
        B, S, H = tokens.shape
        E = expert_weights.shape[0]
        logits = jnp.einsum('bsh,eh->bse', tokens, router_w) + router_b
        probs = jax.nn.softmax(logits, axis=-1)
        top_p, top_i = jax.lax.top_k(probs, TOP_K)
        w = top_p / (jnp.sum(top_p, axis=-1, keepdims=True) + EPS)
        x = tokens.reshape(-1, H)
        idx = top_i.reshape(-1, TOP_K)
        wf = w.reshape(-1, TOP_K)
        y_all = jnp.einsum('nh,ehd->ned', x, expert_weights)
        y_k = jnp.take_along_axis(y_all, idx[:, :, None], axis=1)
        out = jnp.einsum('nk,nkh->nh', wf, y_k)
        acc = jnp.clip(jnp.sum(wf, axis=-1), EPS, None)
        out = (out / acc[:, None]).reshape(B, S, H)
        scale = 1.0 + jnp.sum(w, axis=-1, keepdims=True) * EPS
        return out * scale
    x = L0_attn_x
    x = x + _layernorm(_L0_attn_ref(_layernorm(x, axis=-1), L0_attn_Wq, L0_attn_Wk, L0_attn_Wv, L0_attn_Wa, L0_attn_Wg, L0_attn_Wo, L0_attn_gn_scale, L0_attn_gn_bias, L0_attn_ln1_scale, L0_attn_ln1_bias, L0_attn_W1, L0_attn_b1, L0_attn_W2, L0_attn_b2, L0_attn_ln2_scale, L0_attn_ln2_bias), axis=-1)
    x = x + _layernorm(_L0_ffn_ref(_layernorm(x, axis=-1), L0_ffn_router_w, L0_ffn_router_b, L0_ffn_expert_weights), axis=-1)
    return x

_drawn_inputs = setup_inputs


def setup_inputs(seed=0):
    import zlib

    import numpy as np

    out = dict(_drawn_inputs(seed))
    spreads = {'L0_attn_gn_scale': (1.0, 0.2),
     'L0_attn_gn_bias': (0.0, 0.1),
     'L0_attn_ln1_scale': (1.0, 0.2),
     'L0_attn_ln1_bias': (0.0, 0.1),
     'L0_attn_ln2_scale': (1.0, 0.2),
     'L0_attn_ln2_bias': (0.0, 0.1)}
    factors = {}
    for name, (base, spread) in spreads.items():
        noise = np.random.default_rng([zlib.crc32(name.encode()), seed]).standard_normal(out[name].shape)
        drawn = base * np.exp(spread * noise) if base else spread * noise
        out[name] = jnp.asarray(drawn.astype(out[name].dtype))
    for name, factor in factors.items():
        out[name] = (out[name] * factor).astype(out[name].dtype)
    return out
```

```python
import math
from contextlib import ExitStack

import concourse.bass as bass
from concourse import mybir

F32 = mybir.dt.float32
BF16 = mybir.dt.bfloat16
I32 = mybir.dt.int32
ALU = mybir.AluOpType
ACT = mybir.ActivationFunctionType
AX = mybir.AxisListType

TENSOR = """
turn0/0@0 turn0/1@1 re_a/0@2 turn0/2@3 k/0@4 re_a/1@5 im_a/0@6 im_a/1@7 re_a/2@0 v/0@1 v/1@4 g/0@3 im_a/2@1
turn0/3@6 k/1@7 q/0@2 im_a/3@6 q/1@5 re_a/3@7 v/2@4 k/2@3 cols/0@3 v/3@2 g/1@3 means/0@4 q/2@5 q/3@1 g/2@4 g/3@6
attn/0@0 k/3@7 means/1@3 turn1/0@7 attn/1@4 hidden0/0@3 means/2@6 hidden1/0@2 hidden2/0@0 hidden3/0@5 mlp/0@7
turn1/1@3 attn/2@6 hidden0/1@2 hidden1/1@0 hidden2/1@5 hidden3/1@1 means/3@4 mlp/1@3 turn1/2@7 attn/3@2
hidden0/2@0 hidden1/2@5 turn4/0@1 hidden2/2@4 hidden3/2@6 logits/0@7 mlp/2@3 turn1/3@0 hidden0/3@5 hidden1/3@1
turn4/1@4 hidden2/3@6 hidden3/3@7 logits/1@2 mlp/3@3 turnw/0@5 spread0/0@0 spread1/0@1 spread2/0@4 spread3/0@6
spread4/0@7 spread5/0@2 spread6/0@5 expert0/0@0 turn4/2@3 expert1/0 spread7/0@1 logits/2@3 expert2/0 expert3/0
expert4/0 expert5/0 expert6/0 turnw/1@4 expert7/0 spread0/1@6 spread1/1@7 spread2/1@2 spread3/1@3 spread4/1@5
spread5/1@1 spread6/1@4 expert0/1@6 spread7/1@7 expert1/1 turn4/3@2 expert2/1 expert3/1 logits/3@3 expert4/1
expert5/1 expert6/1 expert7/1 turnw/2@2 spread0/2@5 spread1/2@1 spread2/2@0 spread3/2@4 spread4/2@7 spread5/2@3
spread6/2@2 expert0/2@5 spread7/2@1 expert1/2 expert2/2 expert3/2 turnw/3@0 expert4/2 expert5/2 spread0/3@4
spread1/3@6 spread2/3@7 spread3/3@3 spread4/3@2 spread5/3@0 expert6/2 expert7/2 expert0/3@1 spread6/3@4
spread7/3@6 expert1/3 expert2/3 expert3/3 expert4/3 expert5/3 expert6/3 expert7/3
"""
SCALAR = """
normed0/0 normed0/1 xnT/0 normed0/2 xnT/1 normed0/3 re_sq/0 re_abs/0 k/0 xnT/2 re_sq/1 re_abs/1 im_sq/0 im_sq/1
mag/0 re_abs/2 mag/1 re_sq/2 log/0 im_sq/2 inverse/0 log/1 inverse/1 angle/0 decay/0 angle/1 decay/1 xnT/3
whole/0 k/1 whole/1 frac_abs/0 sine/0 cosine/0 gate/0 im_sq/3 re_sq/3 frac_abs/1 k/2 sine/1 cosine/1 re_norm/0
cols/0 re_abs/3 im_norm/0 mag/2 mag/3 log/2 inverse/2 log/3 re_norm/1 inverse/3 im_norm/1 angle/2 decay/2
angle/3 y_normed/0 decay/3 whole/2 gate/1 frac_abs/2 whole/3 sine/2 k/3 cosine/2 gate/2 gate/3 normed1/0
y_normed/1 frac_abs/3 x1T/0 sine/3 x1bT/0 im_norm/2 re_norm/2 cosine/3 gelu0/0 gelu1/0 gelu2/0 gelu3/0
y_normed/2 normed1/1 im_norm/3 re_norm/3 x1T/1 x1bT/1 gelu0/1 gelu1/1 gelu2/1 gelu3/1 normed1/2 y_normed/3 x1T/2
x1bT/2 normed4/0 gelu0/2 gelu1/2 t4T/0 gelu2/2 gelu3/2 normed1/3 tanh/0 x1T/3 normed4/1 gelu0/3 x1bT/3 gelu1/3
t4T/1 gelu2/3 gelu3/3 tanh/1 wT/0 normed4/2 t4T/2 tanh/2 wT/1 normed4/3 t4T/3 normed5/0 tanh/3 wT/2 normed5/1
wT/3 normed5/2 normed5/3
"""
VECTOR = """
stats0/0 moments0/0 stats0/1 moments0/1 stats0/2 moments0/2 stats0/3 moments0/3 mag2/0 mag2/1 den/0 kv/0 den/1
mag2/2 sign_inv/0 tangent/0 sign_inv/1 tangent/1 sign_mu/0 sum/0 sign_mu/1 sum/1 restart/0 frac/0 kv/1 restart/1
frac/1 kv_sin/0 kv_cos/0 scan_im/0 scan_re/0 mag2/3 q_re/0 kv_sin/1 q_im/0 scan_im/1 im_sums/0 y_parts/0 l1b2/0
den/2 kv_cos/1 kv/2 scan_re/1 den/3 q_re/1 sign_inv/2 q_im/1 tangent/2 sign_inv/3 means/0 tangent/3 im_sums/1
sign_mu/2 sum/2 gated/0 sign_mu/3 sum/3 frac/2 y_parts/1 stats1/0 kv_sin/2 moments1/0 means/1 kv/3 frac/3
kv_cos/2 restart/2 scan_im/2 scan_re/2 restart/3 q_re/2 gated/1 q_im/2 y_parts/2 kv_sin/3 im_sums/2 scan_im/3
stats1/1 means/2 moments1/1 kv_cos/3 scan_re/3 q_re/3 q_im/3 gated/2 y_parts/3 im_sums/3 stats2/0 moments2/0
centre2/0 stats1/2 a2/0 moments1/2 stats3/0 moments3/0 means/3 x2/0 stats4/0 moments4/0 gated/3 stats2/1
moments2/1 centre2/1 stats1/3 a2/1 moments1/3 stats3/1 moments3/1 route0/0 route1/0 x2/1 route2/0 stats4/1
route3/0 moments4/1 route4/0 route5/0 route6/0 route7/0 stats2/2 route8/0 moments2/2 route9/0 centre2/2
route10/0 route11/0 a2/2 route12/0 stats3/2 route13/0 moments3/2 route14/0 route15/0 route16/0 route0/1 route1/1
x2/2 route2/1 stats4/2 route3/1 moments4/2 route4/1 route5/1 route6/1 route7/1 route8/1 stats2/3 route9/1
moments2/3 route10/1 weigh0/0 route11/1 centre2/3 weigh1/0 route12/1 a2/3 route13/1 weigh2/0 stats3/3 route0/2
weigh3/0 moments3/3 weigh4/0 route14/1 weigh5/0 route15/1 route1/2 weigh6/0 route16/1 x2/3 weigh7/0 route2/2
stats4/3 route3/2 moments4/3 route4/2 stats5/0 route5/2 weigh0/1 route6/2 weigh1/1 route7/2 moments5/0 weigh2/1
route8/2 weigh3/1 route9/2 weigh4/1 route10/2 weigh5/1 route11/2 weigh6/1 route12/2 weigh7/1 route13/2 route0/3
route14/2 route1/3 route15/2 route2/3 route16/2 route3/3 route4/3 route5/3 route6/3 route7/3 route8/3 route9/3
route10/3 stats5/1 route11/3 moments5/1 route12/3 route13/3 weigh0/2 route14/3 weigh1/2 route15/3 weigh2/2
route16/3 weigh3/2 weigh4/2 weigh5/2 weigh6/2 weigh7/2 weigh0/3 weigh1/3 weigh2/3 weigh3/3 stats5/2 weigh4/3
moments5/2 weigh5/3 weigh6/3 weigh7/3 stats5/3 moments5/3
"""
GPSIMD = """
constants/0 scale0/0 scale0/1 scale0/2 scale0/3 selectors/0 turns/0 turns/1 y/0 factors/0 turns/2 turns/3 y/1
scale1/0 factors/1 y/2 factors/2 scale1/1 y/3 scale2/0 scale1/2 scale3/0 factors/3 scale4/0 scale2/1 scale1/3
scale3/1 scale4/1 scale2/2 scale3/2 split/0 scale4/2 scale2/3 scale3/3 split/1 scale4/3 scale5/0 out/0 split/2
scale5/1 split/3 out/1 scale5/2 out/2 scale5/3 out/3
"""


def steps_of(table):
    found = []
    for word in table.split():
        word, _, bank = word.partition("@")
        step, _, chunk = word.partition("/")
        found.append((step, int(chunk), int(bank) if bank else None))
    return found


def sandwich(nc, x, Wq, Wk, Wv, Wa, Wg, Wo, gn_scale, gn_bias, ln1_scale, ln1_bias,
             W1, b1, W2, b2, ln2_scale, ln2_bias, router_w, router_b, expert_w, out):
    B, S, D = x.shape
    F = W1.shape[1]
    E = expert_w.shape[0]
    P = 128
    GROUP = D // 32
    NF = F // P
    T = B * S // P
    SEQ = 2
    C = B // SEQ
    N = SEQ * S
    TC = N // P
    PARTS = 3
    NORMS = 6
    EPS = [1e-5, 1e-6, 1e-6, 1e-5, 1e-5, 1e-5]
    EPS_GROUP, EPS_MOE = 1e-6, 1e-10
    ROUND = 1.5 * 2.0 ** 23
    TURN = 2 * math.pi * (1 - 2.0 ** -22)
    TINY = 1e-30
    SIGN = -2 ** 31

    pe_steps, act_steps, dve_steps, pool_steps = [steps_of(t) for t in (TENSOR, SCALAR, VECTOR, GPSIMD)]
    bank_of = {(step, c): b for step, c, b in pe_steps if b is not None}

    ctx = ExitStack()
    with ctx:
        def sb(name, shape, dt=F32):
            return ctx.enter_context(nc.sbuf_tensor(name, shape, dt))

        def sem(name):
            return ctx.enter_context(nc.semaphore(name))

        x_tok = sb("x_tok", [P, T, D])
        xn_tok = sb("xn_tok", [P, T, D])
        n1_tok = sb("n1_tok", [P, T, D])
        a2_tok = sb("a2_tok", [P, T, D])
        x2_tok = sb("x2_tok", [P, T, D])
        t4_tok = sb("t4_tok", [P, T, D])
        xnT = sb("xnT", [P, C, N])
        mu = sb("mu", [P, C, N])
        ang = sb("ang", [P, C, N])
        phase = sb("phase", [P, C, N])
        kv = sb("kv", [P, C, N])
        g_re = sb("g_re", [P, C, N])
        g_im = sb("g_im", [P, C, N])
        y_re = sb("y_re", [P, C, N])
        y_part = sb("y_part", [P, C, N])
        gate = sb("gate", [P, C, N])
        waste = sb("waste", [P, 2, N])
        x1T, x1bT = g_re, g_im
        t4T = phase
        cosT, sinT = ang, phase
        o_tok = y_part
        hid = [kv, mu, ang, gate]
        xs = [kv, mu, ang, gate, xnT, y_re, g_re, g_im]

        wq, wk, wv, wg, wo = [sb(n, [P, D]) for n in ("wq", "wk", "wv", "wg", "wo")]
        wa = sb("wa", [P, 2 * D])
        w1 = sb("w1", [P, F])
        w2 = sb("w2", [P, NF, D])
        we = sb("we", [P, E, D])
        NR = 5 + NF + E
        rows = sb("rows", [NR, D])
        cols = sb("cols", [P, NR])
        gn_s, gn_b, l1_s, l1_b, b2_c = [cols[:, i:i + 1] for i in range(5)]
        b1_c = cols[:, 5:5 + NF]
        rwT = cols[:, 5 + NF:NR]
        l1b2 = sb("l1b2", [P, 1])
        s2_bc = sb("s2_bc", [P, D])
        b2_bc = sb("b2_bc", [P, D])
        rb_row = sb("rb_row", [1, TC * E])
        ones = sb("ones", [1, P])
        ident = sb("ident", [P, P])
        ident_b = sb("ident_b", [P, P], BF16)
        groups = sb("groups", [P, P])
        pick = sb("pick", [PARTS * E, E, P], BF16)
        restart = sb("restart", [P, SEQ, S])
        first_e = sb("first_e", [P, TC, E])
        half_pi = sb("half_pi", [P, 1])
        tiny = sb("tiny", [P, 1])
        rounder = sb("rounder", [P, 1])
        power = sb("power", [P, TC])

        bn = sb("bn", [P, NORMS, T, 6])
        mv = sb("mv", [P, NORMS, T, 2])
        veps = sb("veps", [P, NORMS, T])
        rstd = sb("rstd", [P, NORMS, T])
        minus = sb("minus", [P, NORMS, T])
        shift = sb("shift", [P, NORMS, T])
        shift35 = sb("shift35", [P, T])
        gst = sb("gst", [P, C, 2, 3, SEQ])
        gmean = sb("gmean", [P, C, 3, SEQ])
        gvar = sb("gvar", [P, C, SEQ])
        gw = sb("gw", [P, C, 4, SEQ])
        gn_a = sb("gn_a", [P, C, SEQ])
        gn_c = sb("gn_c", [P, C, SEQ])
        ro = sb("ro", [P, C, 12, TC, E])
        r4 = sb("r4", [P, C, 12, TC])
        wsp = sb("wsp", [P, C, TC, PARTS, E], BF16)
        wrest = sb("wrest", [P, C, 2, TC, E])
        wT = sb("wT", [PARTS * E, C, N], BF16)

        ps = ctx.enter_context(nc.psum_tensor("ps", [P, 8, N], F32))

        def bank(step, c):
            return ps[:, bank_of[step, c], :]

        def tiles(b):
            return b.rearrange("p (t d) -> p t d", d=D)

        def tl(c):
            return slice(TC * c, TC * (c + 1))

        def tok(k):
            return slice(P * k, P * (k + 1))

        s_x = [sem(f"x_loaded{c}") for c in range(C)]
        s_wa = sem("wa_loaded")
        s_rows = sem("rows_loaded")
        s_wkv = sem("kv_gq_weights_loaded")
        s_wmlp = sem("mlp_weights_loaded")
        s_wmoe = sem("moe_weights_loaded")
        s_bc = sem("broadcasts_loaded")
        s_out = sem("out_stored")
        ident_ok = sem("identity_made")
        consts = sem("consts_made")
        colsT = sem("cols_in_psum")
        cols_ok = sem("cols_made")
        l1b2_ok = sem("l1b2_made")
        bn_ok = [sem(f"stats{n}_made") for n in range(NORMS)]
        mv_ok = [sem(f"moments{n}_made") for n in range(NORMS)]
        ve_ok = [sem(f"var_eps{n}_made") for n in range(NORMS)]
        rs_ok = [sem(f"rstd{n}_made") for n in range(NORMS)]
        sh_ok = [sem(f"shift{n}_made") for n in range(NORMS)]
        sh35_ok = sem("shift35_made")
        xn_ok = sem("xn_made")
        xnT_ps = sem("xnT_in_psum")
        xnT_ok = sem("xnT_made")
        ar_ps = sem("re_a_in_psum")
        ai_ps = sem("im_a_in_psum")
        sqr_ok = sem("re_square_made")
        sqi_ok = sem("im_square_made")
        absre_ok = sem("abs_re_made")
        mag2_ok = sem("mag2_made")
        mag_ok = sem("mag_made")
        den_ok = sem("den_made")
        ln_ok = sem("log_made")
        inv_ok = sem("inverse_made")
        sinv_ok = sem("signed_inverse_made")
        tan_ok = sem("tangent_made")
        sig_ok = sem("sigmoid_made")
        ang_ok = sem("angle_made")
        smu_ok = sem("signed_decay_made")
        mu_ok = sem("decay_restarts_made")
        turn_ok = sem("turns_made")
        sum_ok = sem("phase_summed")
        whole_ok = sem("whole_turns_made")
        frac_ok = sem("phase_wrapped")
        k_ps = sem("k_in_psum")
        v_ps = sem("v_in_psum")
        k_ok = sem("k_copied")
        kv_ok = sem("kv_made")
        g_ps = sem("g_in_psum")
        q_ps = sem("q_in_psum")
        sin_ok = sem("sine_made")
        abs_ok = sem("abs_phase_made")
        cos_ok = sem("cosine_made")
        gate_ok = sem("gate_made")
        kc_ok = sem("kv_cos_made")
        ks_ok = sem("kv_sin_made")
        scr_ok = sem("re_scanned")
        sci_ok = sem("im_scanned")
        qr_ok = sem("q_times_re")
        qi_ok = sem("q_times_im")
        pr_ok = sem("y_parts_made")
        pi_ok = sem("im_sums_made")
        nr_ok = sem("re_square_sums_made")
        ni_ok = sem("im_square_sums_made")
        y_ok = sem("y_made")
        gm_ps = sem("group_means_in_psum")
        gm_ok = sem("group_means_made")
        mk = sem("constant_steps")
        gp = sem("group_norm_steps")
        vs = sem("group_variance_steps")
        gn_ok = sem("group_norm_factors_made")
        yn_ok = sem("y_normed")
        z_ok = sem("y_gated")
        o_ps = sem("attention_out_in_psum")
        n1_ok = sem("n1_made")
        n1T_ps = sem("n1T_in_psum")
        x1T_ok = sem("x1T_made")
        x1b_ok = sem("x1bT_made")
        h_ps = sem("hidden_in_psum")
        h_ok = sem("hidden_made")
        m_ps = sem("mlp_out_in_psum")
        u2_ok = sem("norm2_centred")
        a2_ok = sem("a2_made")
        x2_ok = sem("x2_made")
        t4_ok = sem("t4_made")
        t4T_ps = sem("t4T_in_psum")
        t4T_ok = sem("t4T_made")
        lg_ps = sem("logits_in_psum")
        rt = [sem(f"route{n}_done") for n in range(17)]
        th_ok = sem("tanh_made")
        w_ok = sem("token_weights_made")
        sp = sem("split_steps")
        wsp_ok = sem("token_weights_split")
        wT_ps = sem("wT_in_psum")
        wT_ok = sem("wT_made")
        wb_ps = sem("weights_spread")
        xs_ok = sem("tokens_weighted")
        e_ps = sem("experts_in_psum")
        o_ok = sem("experts_normed")
        out_ok = [sem(f"out{c}_made") for c in range(C)]

        block = ctx.enter_context(nc.Block())

        @block.sync
        def _(sync):
            xt = x.rearrange("b s d -> (b s) d").rearrange("(t p) d -> p t d", p=P)
            ot = out.rearrange("b s d -> (b s) d").rearrange("(t p) d -> p t d", p=P)
            for c in range(C):
                sync.dma_start(x_tok[:, tl(c), :], xt[:, tl(c), :]).then_inc(s_x[c], 16)
                if c == 0:
                    sync.dma_start(wa[:, :], Wa).then_inc(s_wa, 16)
                elif c == 1:
                    sync.dma_start(wk[:, :], Wk).then_inc(s_wkv, 16)
                    sync.dma_start(wv[:, :], Wv).then_inc(s_wkv, 16)
                elif c == 2:
                    sync.dma_start(wg[:, :], Wg).then_inc(s_wkv, 16)
                    sync.dma_start(wq[:, :], Wq).then_inc(s_wkv, 16)
            for i, v in enumerate((gn_scale, gn_bias, ln1_scale, ln1_bias, b2)):
                sync.dma_start(rows[i:i + 1, :], v.rearrange("(a d) -> a d", a=1)).then_inc(s_rows, 16)
            sync.dma_start(rows[5:5 + NF, :], b1.rearrange("(f d) -> f d", d=P)).then_inc(s_rows, 16)
            sync.dma_start(rows[5 + NF:NR, :], router_w).then_inc(s_rows, 16)
            sync.dma_start(wo[:, :], Wo).then_inc(s_wmlp, 16)
            sync.dma_start(w1[:, :], W1).then_inc(s_wmlp, 16)
            sync.dma_start(w2[:, :, :], W2.rearrange("(f p) d -> p f d", p=P)).then_inc(s_wmlp, 16)
            sync.dma_start(we[:, :, :], expert_w.rearrange("e h d -> h e d")).then_inc(s_wmoe, 16)
            sync.dma_start(s2_bc[:, :], ln2_scale.partition_broadcast(P)).then_inc(s_bc, 16)
            sync.dma_start(b2_bc[:, :], ln2_bias.partition_broadcast(P)).then_inc(s_bc, 16)
            sync.dma_start(rb_row[:, :].rearrange("p (t e) -> p t e", e=E),
                           router_b.rearrange("(a b e) -> a b e", a=1, b=1).to_broadcast([1, TC, E])).then_inc(s_bc, 16)
            for c in range(C):
                sync.wait_ge(out_ok[c], 1)
                sync.dma_start(ot[:, tl(c), :], tiles(o_tok[:, c, :])).then_inc(s_out, 16)
            sync.wait_ge(s_out, 16 * C)

        @block.gpsimd
        def _(pool):
            pool.memset(ident[:, :], 0.0).then_inc(mk, 1)
            pool.memset(power[:, :], -0.5)
            pool.memset(tiny[:, :], TINY)
            pool.wait_ge(mk, 1)
            pool.affine_select(out=ident[:, :], in_=ident[:, :], compare_op=ALU.not_equal, fill=1.0,
                               base=0, pattern=[[-1, P]], channel_multiplier=1).then_inc(ident_ok, 1)

            for step, c, _ in pool_steps:
                if step == "constants":
                    pool.memset(restart[:, :, :], 1.0).then_inc(mk, 1)
                    pool.memset(groups[:, :], 1.0 / (GROUP * S)).then_inc(mk, 1)
                    pool.memset(pick[:, :, :], 0.0).then_inc(mk, 1)
                    pool.memset(first_e[:, :, :], 1.0).then_inc(mk, 1)
                    pool.memset(half_pi[:, :], math.pi / 2)
                    pool.memset(rounder[:, :], ROUND)
                    pool.memset(ones[:, :], 1.0)
                    pool.wait_ge(mk, 5)
                    pool.memset(first_e[:, :, 0:1], 0.0)
                    pool.memset(restart[:, :, 0:1], 0.0).then_inc(consts, 1)
                    gv = groups[:, :].rearrange("p (g j) -> p g j", j=GROUP)
                    pool.affine_select(out=gv, in_=gv, compare_op=ALU.is_ge, fill=0.0, base=0,
                                       pattern=[[-GROUP, D // GROUP], [0, GROUP]],
                                       channel_multiplier=1).then_inc(mk, 1)
                    pool.wait_ge(mk, 6)
                    pool.affine_select(out=gv, in_=gv, compare_op=ALU.is_ge, fill=0.0, base=GROUP - 1,
                                       pattern=[[GROUP, D // GROUP], [0, GROUP]],
                                       channel_multiplier=-1).then_inc(consts, 1)
                elif step == "selectors":
                    for n in range(PARTS):
                        pool.affine_select(out=pick[:, :, :], in_=pick[:, :, :], compare_op=ALU.not_equal,
                                           fill=1.0, base=-E * n, pattern=[[-1, E], [0, P]],
                                           channel_multiplier=1).then_inc(mk, 1)
                        pool.wait_ge(mk, 7 + n)
                    pool.tensor_copy(ident_b[:, :], ident[:, :]).then_inc(consts, 1)
                elif step.startswith("scale"):
                    n = int(step[5:])
                    pool.wait_ge(mv_ok[n], c + 1)
                    pool.tensor_scalar(veps[:, n, tl(c)], mv[:, n, tl(c), 1], 1.0, EPS[n],
                                       ALU.mult, ALU.add).then_inc(ve_ok[n], 1)
                    pool.tensor_scalar(minus[:, n, tl(c)], mv[:, n, tl(c), 0], -1.0, 0.0,
                                       ALU.mult, ALU.add)
                    pool.wait_ge(ve_ok[n], c + 1)
                    pool.tensor_tensor(rstd[:, n, tl(c)], veps[:, n, tl(c)], power[:, :],
                                       ALU.pow).then_inc(rs_ok[n], 1)
                    if n != 2:
                        pool.wait_ge(rs_ok[n], c + 1)
                        pool.tensor_tensor(shift[:, n, tl(c)], minus[:, n, tl(c)], rstd[:, n, tl(c)],
                                           ALU.mult).then_inc(sh_ok[n], 1)
                    if n == 5:
                        pool.wait_ge(sh_ok[5], c + 1)
                        pool.tensor_tensor(shift35[:, tl(c)], shift[:, 3, tl(c)], shift[:, 5, tl(c)],
                                           ALU.add).then_inc(sh35_ok, 1)
                elif step == "turns":
                    pool.wait_ge(ang_ok, c + 1)
                    pool.tensor_scalar(ang[:, c, :], ang[:, c, :], 1.0 / math.pi, 0.0,
                                       ALU.mult, ALU.add).then_inc(turn_ok, 1)
                elif step == "factors":
                    pool.wait_ge(gm_ok, c + 1)
                    m, w = gmean[:, c], gw[:, c]
                    pool.tensor_tensor(w[:, 2, :], gvar[:, c, :], power[:, 0:SEQ], ALU.pow).then_inc(gp, 1)
                    pool.wait_ge(gp, 3 * c + 1)
                    pool.tensor_tensor(gn_a[:, c, :], w[:, 2, :], gn_s.to_broadcast([P, SEQ]), ALU.mult).then_inc(gp, 1)
                    pool.wait_ge(gp, 3 * c + 2)
                    pool.tensor_tensor(w[:, 3, :], m[:, 0, :], gn_a[:, c, :], ALU.mult).then_inc(gp, 1)
                    pool.wait_ge(gp, 3 * c + 3)
                    pool.tensor_tensor(gn_c[:, c, :], gn_b.to_broadcast([P, SEQ]), w[:, 3, :],
                                       ALU.subtract).then_inc(gn_ok, 1)
                elif step == "y":
                    pool.wait_ge(pr_ok, 2 * SEQ * (c + 1))
                    pool.tensor_tensor(y_re[:, c, :], y_re[:, c, :], y_part[:, c, :], ALU.add).then_inc(y_ok, 1)
                elif step == "out":
                    pool.wait_ge(o_ok, c + 1)
                    pool.tensor_tensor(tiles(o_tok[:, c, :]), tiles(o_tok[:, c, :]), x2_tok[:, tl(c), :],
                                       ALU.add).then_inc(out_ok[c], 1)
                elif step == "split":
                    pool.wait_ge(w_ok, c + 1)
                    w = ro[:, c, 11]
                    rest = w
                    for n in range(PARTS - 1):
                        pool.tensor_copy(wsp[:, c, :, n, :], rest).then_inc(sp, 1)
                        pool.wait_ge(sp, 2 * (PARTS - 1) * c + 2 * n + 1)
                        pool.tensor_tensor(wrest[:, c, n], rest, wsp[:, c, :, n, :], ALU.subtract).then_inc(sp, 1)
                        pool.wait_ge(sp, 2 * (PARTS - 1) * c + 2 * n + 2)
                        rest = wrest[:, c, n]
                    pool.tensor_copy(wsp[:, c, :, PARTS - 1, :], rest).then_inc(wsp_ok, 1)

        @block.tensor
        def _(pe):
            def reader(step, c):
                one = {"cols": cols_ok, "turn0": xnT_ok, "re_a": smu_ok, "im_a": tan_ok, "k": k_ok, "v": kv_ok,
                       "g": gate_ok, "q": qi_ok, "means": gm_ok, "attn": n1_ok, "turn1": x1b_ok, "mlp": u2_ok,
                       "turn4": t4T_ok, "logits": rt[1], "turnw": wT_ok, "expert0": o_ok}
                if step in one:
                    return one[step], c + 1
                kind, n = step[:-1], int(step[-1])
                return (h_ok, NF * c + n + 1) if kind == "hidden" else (xs_ok, E * c + n + 1)

            held = {}

            def turn(b, src, c, done):
                for k in range(TC):
                    ins = pe.transpose(b[:, tok(k)], src[:, TC * c + k, :], ident[:, :])
                ins.then_inc(done, 1)

            for step, c, b in pe_steps:
                if b is not None:
                    if b in held:
                        pe.wait_ge(*reader(*held[b]))
                    held[b] = (step, c)
                if step == "cols":
                    pe.wait_ge(s_rows, 16 * 7)
                    pe.wait_ge(ident_ok, 1)
                    pe.transpose(bank("cols", 0)[:, 0:NR], rows[:, :], ident[0:NR, 0:NR]).then_inc(colsT, 1)
                elif step == "turn0":
                    pe.wait_ge(ident_ok, 1)
                    pe.wait_ge(xn_ok, c + 1)
                    turn(bank("turn0", c), xn_tok, c, xnT_ps)
                elif step == "re_a":
                    pe.wait_ge(s_wa, 16)
                    pe.wait_ge(xnT_ok, c + 1)
                    pe.matmul(bank("re_a", c), wa[:, 0:D], xnT[:, c, :], start=True, stop=True).then_inc(ar_ps, 1)
                elif step == "im_a":
                    pe.wait_ge(xnT_ok, c + 1)
                    pe.matmul(bank("im_a", c), wa[:, D:2 * D], xnT[:, c, :], start=True, stop=True).then_inc(ai_ps, 1)
                elif step in ("k", "v", "g", "q"):
                    w, done = {"k": (wk, k_ps), "v": (wv, v_ps), "g": (wg, g_ps), "q": (wq, q_ps)}[step]
                    pe.wait_ge(s_wkv, 16 * 4)
                    pe.wait_ge(xnT_ok, c + 1)
                    pe.matmul(bank(step, c), w[:, :], xnT[:, c, :], start=True, stop=True).then_inc(done, 1)
                elif step == "means":
                    pe.wait_ge(consts, 2)
                    pe.wait_ge(pr_ok, 2 * SEQ * (c + 1))
                    pe.wait_ge(pi_ok, 2 * SEQ * (c + 1))
                    pe.wait_ge(nr_ok, SEQ * (c + 1))
                    pe.wait_ge(ni_ok, SEQ * (c + 1))
                    for n in range(2):
                        ins = pe.matmul(bank("means", c)[:, 0:3 * SEQ], groups[:, :],
                                        gst[:, c, n].rearrange("p k s -> p (k s)"), start=(n == 0), stop=(n == 1))
                    ins.then_inc(gm_ps, 1)
                elif step == "attn":
                    pe.wait_ge(s_wmlp, 16 * 3)
                    pe.wait_ge(z_ok, c + 1)
                    for k in range(TC):
                        pe.matmul(bank("attn", c)[:, tok(k)], xnT[:, c, tok(k)], ident[:, :], start=True, stop=False)
                        ins = pe.matmul(bank("attn", c)[:, tok(k)], y_re[:, c, tok(k)], wo[:, :],
                                        start=False, stop=True)
                    ins.then_inc(o_ps, 1)
                elif step == "turn1":
                    pe.wait_ge(n1_ok, c + 1)
                    turn(bank("turn1", c), n1_tok, c, n1T_ps)
                elif step.startswith("hidden"):
                    f = int(step[-1])
                    pe.wait_ge(x1T_ok, c + 1)
                    pe.matmul(bank(step, c), w1[:, P * f:P * (f + 1)], x1T[:, c, :],
                              start=True, stop=True).then_inc(h_ps, 1)
                elif step == "mlp":
                    pe.wait_ge(x1b_ok, c + 1)
                    pe.wait_ge(h_ok, NF * (c + 1))
                    for k in range(TC):
                        pe.matmul(bank("mlp", c)[:, tok(k)], x1bT[:, c, tok(k)], ident[:, :],
                                  start=True, stop=False)
                        for f in range(NF):
                            ins = pe.matmul(bank("mlp", c)[:, tok(k)], hid[f][:, c, tok(k)], w2[:, f, :],
                                            start=False, stop=(f == NF - 1))
                    ins.then_inc(m_ps, 1)
                elif step == "turn4":
                    pe.wait_ge(t4_ok, c + 1)
                    turn(bank("turn4", c), t4_tok, c, t4T_ps)
                elif step == "logits":
                    pe.wait_ge(t4T_ok, c + 1)
                    pe.wait_ge(consts, 1)
                    pe.wait_ge(s_bc, 16 * 3)
                    pe.matmul(bank("logits", c)[:, 0:TC * E], ones[:, :], rb_row[:, :], start=True, stop=False,
                              skip_group_check=True)
                    for k in range(TC):
                        ins = pe.matmul(bank("logits", c)[:, E * k:E * (k + 1)], t4T[:, c, tok(k)], rwT,
                                        start=False, stop=True, skip_group_check=True)
                    ins.then_inc(lg_ps, 1)
                elif step == "turnw":
                    pe.wait_ge(consts, 3)
                    pe.wait_ge(wsp_ok, c + 1)
                    for k in range(TC):
                        ins = pe.transpose(bank("turnw", c).bitcast(BF16)[0:PARTS * E, tok(k)],
                                           wsp[:, c, k].rearrange("p n e -> p (n e)"), ident_b[:, :])
                    ins.then_inc(wT_ps, 1)
                elif step.startswith("spread"):
                    e = int(step[-1])
                    pe.wait_ge(wT_ok, c + 1)
                    pe.matmul(bank(step, c), pick[:, e, :], wT[:, c, :], start=True, stop=True).then_inc(wb_ps, 1)
                elif step.startswith("expert"):
                    e = int(step[-1])
                    pe.wait_ge(s_wmoe, 16)
                    pe.wait_ge(xs_ok, E * c + e + 1)
                    for k in range(TC):
                        ins = pe.matmul(bank("expert0", c)[:, tok(k)], xs[e][:, c, tok(k)], we[:, e, :],
                                        start=(e == 0 and k == 0), stop=(e == E - 1), skip_group_check=True)
                    ins.then_inc(e_ps, 1)

        @block.scalar
        def _(act):
            tables = {"mag": "sqrt_and_others", "log": "natural_log_exp_and_others",
                      "inverse": "natural_log_exp_and_others", "decay": "sigmoid_and_others",
                      "angle": "sigmoid_and_others", "gate": "silu_and_others", "cosine": "silu_and_others",
                      "sine": "silu_and_others", "tanh": "gelu_apprx_tanh_and_others"}
            tables |= {f"gelu{f}": "gelu_apprx_tanh_and_others" for f in range(NF)}
            loaded = "sqrt_and_others"
            act.preload_act_table_set(loaded)

            def normed(n, c, dst, tile_of, done):
                act.wait_ge(sh_ok[n], c + 1)
                for k in range(TC):
                    t = TC * c + k
                    ins = act.activation(dst[:, t, :], tile_of(k), ACT.Identity,
                                         scale=rstd[:, n, t:t + 1], bias=shift[:, n, t:t + 1])
                ins.then_inc(done, 1)

            for step, c, _ in act_steps:
                if tables.get(step, loaded) != loaded:
                    loaded = tables[step]
                    act.preload_act_table_set(loaded)
                if step == "cols":
                    act.wait_ge(colsT, 1)
                    act.activation(cols[:, :], bank("cols", 0)[:, 0:NR], ACT.Copy).then_inc(cols_ok, 1)
                elif step == "normed0":
                    act.wait_ge(s_x[c], 16)
                    normed(0, c, xn_tok, lambda k: x_tok[:, TC * c + k, :], xn_ok)
                elif step == "xnT":
                    act.wait_ge(xnT_ps, c + 1)
                    act.activation(xnT[:, c, :], bank("turn0", c), ACT.Copy).then_inc(xnT_ok, 1)
                elif step == "re_sq":
                    act.wait_ge(ar_ps, c + 1)
                    act.activation(mu[:, c, :], bank("re_a", c), ACT.Square).then_inc(sqr_ok, 1)
                elif step == "im_sq":
                    act.wait_ge(ai_ps, c + 1)
                    act.activation(ang[:, c, :], bank("im_a", c), ACT.Square).then_inc(sqi_ok, 1)
                elif step == "re_abs":
                    act.wait_ge(ar_ps, c + 1)
                    act.activation(y_part[:, c, :], bank("re_a", c), ACT.Abs).then_inc(absre_ok, 1)
                elif step == "mag":
                    act.wait_ge(mag2_ok, c + 1)
                    act.wait_ge(ident_ok, 1)
                    act.activation(mu[:, c, :], mu[:, c, :], ACT.Sqrt, bias=tiny[:, :]).then_inc(mag_ok, 1)
                elif step == "log":
                    act.wait_ge(den_ok, c + 1)
                    act.activation(ang[:, c, :], ang[:, c, :], ACT.Ln).then_inc(ln_ok, 1)
                elif step == "inverse":
                    act.wait_ge(ln_ok, c + 1)
                    act.activation(ang[:, c, :], ang[:, c, :], ACT.Exp, scale=-1.0).then_inc(inv_ok, 1)
                elif step == "decay":
                    act.wait_ge(den_ok, c + 1)
                    act.activation(mu[:, c, :], mu[:, c, :], ACT.Sigmoid).then_inc(sig_ok, 1)
                elif step == "angle":
                    act.wait_ge(tan_ok, c + 1)
                    act.activation(ang[:, c, :], ang[:, c, :], ACT.Arctan).then_inc(ang_ok, 1)
                elif step == "whole":
                    act.wait_ge(sum_ok, c + 1)
                    act.wait_ge(consts, 1)
                    act.activation(ang[:, c, :], phase[:, c, :], ACT.Identity, bias=rounder[:, :]).then_inc(whole_ok, 1)
                elif step == "k":
                    act.wait_ge(k_ps, c + 1)
                    act.activation(kv[:, c, :], bank("k", c), ACT.Copy).then_inc(k_ok, 1)
                elif step == "gate":
                    act.wait_ge(g_ps, c + 1)
                    act.activation(gate[:, c, :], bank("g", c), ACT.Silu).then_inc(gate_ok, 1)
                elif step == "frac_abs":
                    act.wait_ge(frac_ok, c + 1)
                    act.activation(cosT[:, c, :], phase[:, c, :], ACT.Abs).then_inc(abs_ok, 1)
                elif step == "cosine":
                    act.wait_ge(abs_ok, c + 1)
                    act.activation(cosT[:, c, :], cosT[:, c, :], ACT.Sin, scale=-TURN,
                                   bias=half_pi[:, :]).then_inc(cos_ok, 1)
                elif step == "sine":
                    act.wait_ge(abs_ok, c + 1)
                    act.activation(sinT[:, c, :], phase[:, c, :], ACT.Sin, scale=-TURN).then_inc(sin_ok, 1)
                elif step in ("re_norm", "im_norm"):
                    n, g, ready, done = (0, g_re, qr_ok, nr_ok) if step == "re_norm" else (1, g_im, qi_ok, ni_ok)
                    act.wait_ge(ready, c + 1)
                    if c >= 1:
                        act.wait_ge(done, SEQ * c)
                    for s in range(SEQ):
                        t = slice(s * S, (s + 1) * S)
                        act.activation(waste[:, n, t], g[:, c, t], ACT.Square,
                                       accum_out=gst[:, c, n, 2, s:s + 1]).then_inc(done, 1)
                elif step == "y_normed":
                    act.wait_ge(gn_ok, c + 1)
                    act.wait_ge(y_ok, c + 1)
                    for s in range(SEQ):
                        t = slice(s * S, (s + 1) * S)
                        ins = act.activation(y_re[:, c, t], y_re[:, c, t], ACT.Identity,
                                             scale=gn_a[:, c, s:s + 1], bias=gn_c[:, c, s:s + 1])
                    ins.then_inc(yn_ok, 1)
                elif step == "normed1":
                    normed(1, c, n1_tok, lambda k: bank("attn", c)[:, tok(k)], n1_ok)
                elif step == "x1T":
                    act.wait_ge(n1T_ps, c + 1)
                    act.wait_ge(cols_ok, 1)
                    act.activation(x1T[:, c, :], bank("turn1", c), ACT.Identity, scale=l1_s, bias=l1_b).then_inc(x1T_ok, 1)
                elif step == "x1bT":
                    act.wait_ge(l1b2_ok, 1)
                    act.wait_ge(n1T_ps, c + 1)
                    act.activation(x1bT[:, c, :], bank("turn1", c), ACT.Identity, scale=l1_s,
                                   bias=l1b2[:, :]).then_inc(x1b_ok, 1)
                elif step.startswith("gelu"):
                    f = int(step[-1])
                    act.wait_ge(h_ps, NF * c + f + 1)
                    act.activation(hid[f][:, c, :], bank(f"hidden{f}", c), ACT.Gelu_apprx_tanh,
                                   bias=b1_c[:, f:f + 1]).then_inc(h_ok, 1)
                elif step == "normed4":
                    act.wait_ge(x2_ok, c + 1)
                    normed(4, c, t4_tok, lambda k: x2_tok[:, TC * c + k, :], t4_ok)
                elif step == "t4T":
                    act.wait_ge(t4T_ps, c + 1)
                    act.activation(t4T[:, c, :], bank("turn4", c), ACT.Copy).then_inc(t4T_ok, 1)
                elif step == "tanh":
                    act.wait_ge(rt[1], c + 1)
                    act.activation(ro[:, c, 1], ro[:, c, 0], ACT.Tanh, scale=0.5).then_inc(th_ok, 1)
                elif step == "wT":
                    act.wait_ge(wT_ps, c + 1)
                    act.activation(wT[:, c, :], bank("turnw", c).bitcast(BF16)[0:PARTS * E, 0:N],
                                   ACT.Copy).then_inc(wT_ok, 1)
                elif step == "normed5":
                    act.wait_ge(sh35_ok, c + 1)
                    for k in range(TC):
                        t = TC * c + k
                        ins = act.activation(tiles(o_tok[:, c, :])[:, k, :], bank("expert0", c)[:, tok(k)],
                                             ACT.Identity, scale=rstd[:, 5, t:t + 1], bias=shift35[:, t:t + 1])
                    ins.then_inc(o_ok, 1)

        @block.vector
        def _(dve):
            def over_e(v):
                return v.unsqueeze(2).to_broadcast([P, TC, E])

            def stats(n, c, ready, count, tile_of):
                dve.wait_ge(ready, count)
                for k in range(TC):
                    ins = dve.bn_stats(bn[:, n, TC * c + k, :], tile_of(k))
                ins.then_inc(bn_ok[n], 1)

            for step, c, _ in dve_steps:
                if step == "l1b2":
                    dve.wait_ge(cols_ok, 1)
                    dve.tensor_tensor(l1b2[:, :], l1_b, b2_c, ALU.add).then_inc(l1b2_ok, 1)
                elif step == "stats0":
                    stats(0, c, s_x[c], 16, lambda k: x_tok[:, TC * c + k, :])
                elif step == "stats1":
                    stats(1, c, o_ps, c + 1, lambda k: bank("attn", c)[:, tok(k)])
                elif step == "stats2":
                    stats(2, c, m_ps, c + 1, lambda k: bank("mlp", c)[:, tok(k)])
                elif step == "stats3":
                    stats(3, c, a2_ok, c + 1, lambda k: a2_tok[:, TC * c + k, :])
                elif step == "stats4":
                    stats(4, c, x2_ok, c + 1, lambda k: x2_tok[:, TC * c + k, :])
                elif step == "stats5":
                    stats(5, c, e_ps, E * (c + 1), lambda k: bank("expert0", c)[:, tok(k)])
                elif step.startswith("moments"):
                    n = int(step[-1])
                    dve.wait_ge(bn_ok[n], c + 1)
                    for k in range(TC):
                        ins = dve.bn_aggr(mv[:, n, TC * c + k, :], bn[:, n, TC * c + k, :])
                    ins.then_inc(mv_ok[n], 1)
                elif step == "mag2":
                    dve.wait_ge(sqr_ok, c + 1)
                    dve.wait_ge(sqi_ok, c + 1)
                    dve.tensor_tensor(mu[:, c, :], mu[:, c, :], ang[:, c, :], ALU.add).then_inc(mag2_ok, 1)
                elif step == "den":
                    dve.wait_ge(mag_ok, c + 1)
                    dve.wait_ge(absre_ok, c + 1)
                    dve.tensor_tensor(ang[:, c, :], y_part[:, c, :], mu[:, c, :], ALU.add).then_inc(den_ok, 1)
                elif step == "sign_inv":
                    dve.wait_ge(inv_ok, c + 1)
                    dve.scalar_tensor_tensor(out=ang[:, c, :].bitcast(I32), in0=bank("re_a", c).bitcast(I32),
                                             scalar=SIGN, in1=ang[:, c, :].bitcast(I32),
                                             op0=ALU.bitwise_and, op1=ALU.bitwise_or).then_inc(sinv_ok, 1)
                elif step == "tangent":
                    dve.wait_ge(sinv_ok, c + 1)
                    dve.tensor_tensor(ang[:, c, :], bank("im_a", c), ang[:, c, :], ALU.mult).then_inc(tan_ok, 1)
                elif step == "sign_mu":
                    dve.wait_ge(sig_ok, c + 1)
                    dve.scalar_tensor_tensor(out=mu[:, c, :].bitcast(I32), in0=bank("re_a", c).bitcast(I32),
                                             scalar=SIGN, in1=mu[:, c, :].bitcast(I32),
                                             op0=ALU.bitwise_and, op1=ALU.bitwise_or).then_inc(smu_ok, 1)
                elif step == "restart":
                    dve.wait_ge(smu_ok, c + 1)
                    dve.memset(mu[:, c, :].rearrange("p (s t) -> p s t", t=S)[:, :, 0:1], 0.0).then_inc(mu_ok, 1)
                elif step == "sum":
                    dve.wait_ge(consts, 1)
                    dve.wait_ge(turn_ok, c + 1)
                    dve.tensor_tensor_scan(phase[:, c, :], restart[:, :, :].rearrange("p s t -> p (s t)"),
                                           ang[:, c, :], 0.0, ALU.mult, ALU.add).then_inc(sum_ok, 1)
                elif step == "frac":
                    dve.wait_ge(whole_ok, c + 1)
                    dve.scalar_tensor_tensor(out=phase[:, c, :], in0=ang[:, c, :], scalar=ROUND,
                                             in1=phase[:, c, :], op0=ALU.subtract,
                                             op1=ALU.subtract).then_inc(frac_ok, 1)
                elif step == "kv":
                    dve.wait_ge(v_ps, c + 1)
                    dve.wait_ge(k_ok, c + 1)
                    dve.tensor_tensor(kv[:, c, :], bank("v", c), kv[:, c, :], ALU.mult).then_inc(kv_ok, 1)
                elif step == "kv_cos":
                    dve.wait_ge(kv_ok, c + 1)
                    dve.wait_ge(cos_ok, c + 1)
                    dve.tensor_tensor(g_re[:, c, :], kv[:, c, :], cosT[:, c, :], ALU.mult).then_inc(kc_ok, 1)
                elif step == "kv_sin":
                    dve.wait_ge(kv_ok, c + 1)
                    dve.wait_ge(sin_ok, c + 1)
                    dve.tensor_tensor(g_im[:, c, :], kv[:, c, :], sinT[:, c, :], ALU.mult).then_inc(ks_ok, 1)
                elif step in ("scan_re", "scan_im"):
                    g, ready, done = (g_re, kc_ok, scr_ok) if step == "scan_re" else (g_im, ks_ok, sci_ok)
                    dve.wait_ge(mu_ok, c + 1)
                    dve.wait_ge(ready, c + 1)
                    dve.tensor_tensor_scan(g[:, c, :], mu[:, c, :], g[:, c, :], 0.0,
                                           ALU.mult, ALU.add).then_inc(done, 1)
                elif step in ("q_re", "q_im"):
                    g, ready, done = (g_re, scr_ok, qr_ok) if step == "q_re" else (g_im, sci_ok, qi_ok)
                    dve.wait_ge(q_ps, c + 1)
                    dve.wait_ge(ready, c + 1)
                    dve.tensor_tensor(g[:, c, :], bank("q", c), g[:, c, :], ALU.mult).then_inc(done, 1)
                elif step in ("y_parts", "im_sums"):
                    if step == "y_parts":
                        todo, part, done = ((y_re, g_re, cosT, 1.0), (y_part, g_im, sinT, 1.0)), 0, pr_ok
                    else:
                        todo, part, done = ((kv, g_re, sinT, 1.0), (mu, g_im, cosT, -1.0)), 1, pi_ok
                    dve.wait_ge(qr_ok, c + 1)
                    dve.wait_ge(qi_ok, c + 1)
                    for s in range(SEQ):
                        t = slice(s * S, (s + 1) * S)
                        for n, (o, g, w, sign) in enumerate(todo):
                            dve.tensor_tensor_reduce(out=o[:, c, t], in0=g[:, c, t], in1=w[:, c, t], scale=sign,
                                                     scalar=0.0, op0=ALU.mult, op1=ALU.add,
                                                     accum_out=gst[:, c, n, part, s:s + 1]).then_inc(done, 1)
                elif step == "means":
                    dve.wait_ge(gm_ps, c + 1)
                    m = bank("means", c)[:, 0:3 * SEQ].rearrange("p (k s) -> p k s", s=SEQ)
                    dve.tensor_copy(gmean[:, c], m).then_inc(vs, 1)
                    dve.wait_ge(vs, 3 * c + 1)
                    dve.tensor_tensor(gw[:, c, 0:2, :], gmean[:, c, 0:2, :], gmean[:, c, 0:2, :], ALU.mult).then_inc(vs, 1)
                    dve.wait_ge(vs, 3 * c + 2)
                    dve.scalar_tensor_tensor(out=gvar[:, c, :], in0=gmean[:, c, 2, :], scalar=EPS_GROUP,
                                             in1=gw[:, c, 0, :], op0=ALU.add, op1=ALU.subtract).then_inc(vs, 1)
                    dve.wait_ge(vs, 3 * c + 3)
                    dve.tensor_tensor(gvar[:, c, :], gvar[:, c, :], gw[:, c, 1, :], ALU.subtract).then_inc(gm_ok, 1)
                elif step == "gated":
                    dve.wait_ge(gate_ok, c + 1)
                    dve.wait_ge(yn_ok, c + 1)
                    dve.tensor_tensor(y_re[:, c, :], y_re[:, c, :], gate[:, c, :], ALU.mult).then_inc(z_ok, 1)
                elif step == "centre2":
                    if c == 0:
                        dve.wait_ge(s_bc, 16 * 3)
                    dve.wait_ge(mv_ok[2], c + 1)
                    for k in range(TC):
                        t = TC * c + k
                        ins = dve.scalar_tensor_tensor(out=a2_tok[:, t, :], in0=bank("mlp", c)[:, tok(k)],
                                                       scalar=mv[:, 2, t, 0:1], in1=s2_bc[:, :],
                                                       op0=ALU.subtract, op1=ALU.mult)
                    ins.then_inc(u2_ok, 1)
                elif step == "a2":
                    dve.wait_ge(u2_ok, c + 1)
                    dve.wait_ge(rs_ok[2], c + 1)
                    for k in range(TC):
                        t = TC * c + k
                        ins = dve.scalar_tensor_tensor(out=a2_tok[:, t, :], in0=a2_tok[:, t, :],
                                                       scalar=rstd[:, 2, t:t + 1], in1=b2_bc[:, :],
                                                       op0=ALU.mult, op1=ALU.add)
                    ins.then_inc(a2_ok, 1)
                elif step == "x2":
                    dve.wait_ge(rs_ok[3], c + 1)
                    for k in range(TC):
                        t = TC * c + k
                        ins = dve.scalar_tensor_tensor(out=x2_tok[:, t, :], in0=a2_tok[:, t, :],
                                                       scalar=rstd[:, 3, t:t + 1], in1=x_tok[:, t, :],
                                                       op0=ALU.mult, op1=ALU.add)
                    ins.then_inc(x2_ok, 1)
                elif step.startswith("route"):
                    n = int(step[5:])
                    R, Q = ro[:, c], r4[:, c]
                    lg = bank("logits", c)[:, 0:TC * E].rearrange("p (t e) -> p t e", e=E)
                    top = R[:, 2]
                    most, second = top[:, :, 0], top[:, :, 1]
                    if n == 0:
                        dve.wait_ge(lg_ps, c + 1)
                        for k in range(TC):
                            ins = dve.max(top[:, k, :], lg[:, k, :])
                    else:
                        dve.wait_ge(rt[n - 1], c + 1)
                    if n == 1:
                        dve.tensor_tensor(R[:, 3], lg, over_e(second), ALU.is_equal)
                        dve.tensor_tensor(R[:, 4], lg, over_e(second), ALU.is_gt)
                        dve.tensor_tensor(Q[:, 0], most, second, ALU.is_equal)
                        ins = dve.tensor_tensor(R[:, 0], lg, over_e(most), ALU.subtract)
                    elif n == 2:
                        ins = dve.tensor_tensor_scan(R[:, 5].rearrange("p t e -> p (t e)"),
                                                     first_e[:, :, :].rearrange("p t e -> p (t e)"),
                                                     R[:, 3].rearrange("p t e -> p (t e)"), 0.0, ALU.mult, ALU.add)
                    elif n == 3:
                        ins = dve.tensor_tensor(R[:, 5], R[:, 5], over_e(Q[:, 0]), ALU.subtract)
                    elif n == 4:
                        ins = dve.scalar_tensor_tensor(out=R[:, 5], in0=R[:, 5], scalar=1.0, in1=R[:, 3],
                                                       op0=ALU.is_le, op1=ALU.mult)
                    elif n == 5:
                        dve.wait_ge(th_ok, c + 1)
                        dve.tensor_tensor(R[:, 6], R[:, 5], R[:, 4], ALU.add)
                        ins = dve.tensor_scalar(R[:, 7], R[:, 1], -1.0, 1.0, ALU.mult, ALU.add)
                    elif n == 6:
                        ins = dve.reciprocal(R[:, 7], R[:, 7])
                    elif n == 7:
                        ins = dve.scalar_tensor_tensor(out=R[:, 8], in0=R[:, 1], scalar=1.0, in1=R[:, 7],
                                                       op0=ALU.add, op1=ALU.mult)
                    elif n == 8:
                        dve.tensor_reduce(out=Q[:, 1], in_=R[:, 8], op=ALU.add, axis=AX.X)
                        ins = dve.tensor_tensor(R[:, 9], R[:, 8], R[:, 6], ALU.mult)
                    elif n == 9:
                        ins = dve.tensor_reduce(out=Q[:, 2], in_=R[:, 9], op=ALU.add, axis=AX.X)
                    elif n == 10:
                        ins = dve.scalar_tensor_tensor(out=Q[:, 3], in0=Q[:, 1], scalar=EPS_MOE, in1=Q[:, 2],
                                                       op0=ALU.mult, op1=ALU.add)
                    elif n == 11:
                        ins = dve.reciprocal(Q[:, 4], Q[:, 3])
                    elif n == 12:
                        ins = dve.tensor_tensor(Q[:, 5], Q[:, 2], Q[:, 4], ALU.mult)
                    elif n == 13:
                        dve.tensor_scalar(Q[:, 6], Q[:, 5], EPS_MOE, None, ALU.max)
                        ins = dve.tensor_scalar(Q[:, 7], Q[:, 5], EPS_MOE, 1.0, ALU.mult, ALU.add)
                    elif n == 14:
                        dve.reciprocal(Q[:, 8], Q[:, 6])
                        ins = dve.tensor_tensor(Q[:, 9], Q[:, 7], Q[:, 4], ALU.mult)
                    elif n == 15:
                        ins = dve.tensor_tensor(Q[:, 10], Q[:, 9], Q[:, 8], ALU.mult)
                    elif n == 16:
                        ins = dve.tensor_tensor(R[:, 11], R[:, 9], over_e(Q[:, 10]), ALU.mult)
                    ins.then_inc(w_ok if n == 16 else rt[n], 1)
                elif step.startswith("weigh"):
                    e = int(step[-1])
                    dve.wait_ge(m_ps, c + 1)
                    dve.wait_ge(wb_ps, E * c + e + 1)
                    dve.tensor_tensor(xs[e][:, c, :], bank(f"spread{e}", c), t4T[:, c, :],
                                      ALU.mult).then_inc(xs_ok, 1)
                elif step == "out":
                    dve.wait_ge(o_ok, c + 1)
                    dve.tensor_tensor(tiles(o_tok[:, c, :]), tiles(o_tok[:, c, :]), x2_tok[:, tl(c), :],
                                      ALU.add).then_inc(out_ok[c], 1)


_INS = ['x', 'Wq', 'Wk', 'Wv', 'Wa', 'Wg', 'Wo', 'gn_scale', 'gn_bias', 'ln1_scale', 'ln1_bias',
        'W1', 'b1', 'W2', 'b2', 'ln2_scale', 'ln2_bias']
_INS = ["L0_attn_" + n for n in _INS] + ["L0_ffn_" + n for n in ('router_w', 'router_b', 'expert_weights')]
_OUTS = [((8, 256, 128), 'float32')]


def kernel(**inputs):
    import numpy as _np
    import concourse.bacc as _bacc
    from concourse import mybir as _mybir
    from concourse.bass_utils import run_bass_kernel_spmd as _run

    nc = _bacc.Bacc("TRN2", target_bir_lowering=False, num_devices=1)
    arrays, args = {}, []
    for name in _INS:
        a = _np.ascontiguousarray(inputs[name])
        arrays[f"in_{name}_dram"] = a
        args.append(nc.dram_tensor(f"in_{name}_dram", a.shape, _mybir.dt.from_np(a.dtype), kind="ExternalInput").ap())
    for i, (shape, dtype) in enumerate(_OUTS):
        dt = _mybir.dt.from_np(_np.dtype(dtype))
        args.append(nc.dram_tensor(f"out_{i}_dram", shape, dt, kind="ExternalOutput").ap())
    sandwich(nc, *args)
    r = _run(nc, [arrays], core_ids=[0])
    got = tuple(r.results[0][f"out_{i}_dram"] for i in range(len(_OUTS)))
    return got[0]
```

```python
import math
from contextlib import ExitStack

import concourse.bass as bass
from concourse import mybir

F32 = mybir.dt.float32
BF16 = mybir.dt.bfloat16
I32 = mybir.dt.int32
ALU = mybir.AluOpType
ACT = mybir.ActivationFunctionType
AX = mybir.AxisListType

TENSOR = """
warm/0@7 turn0/0@0 re_a/0@1 im_a/0@2 turn0/1@3 v/0@4 im_a/1@5 re_a/1@6 k/0@7 k/1@0 turn0/2@3 v/1@7 im_a/2@3
re_a/2@2 turn0/3@4 q/0@5 g/0@0 re_a/3@7 cols/0@4 k/2@1 im_a/3@6 k/3@0 q/1@5 means/0@1 g/1@5 q/2@4 q/3@0 g/2@1
means/1@3 attn/0@6 g/3@5 v/2@1 attn/1@3 turn1/0@1 v/3@2 hidden0/0@6 hidden1/0@5 mlpx/0@7 hidden2/0@1 mlp0/0
mlp1/0 means/2@4 hidden3/0@6 turn1/1@5 mlp2/0 mlp3/0 hidden0/1@2 hidden1/1@3 hidden2/1@1 attn/2@4 hidden3/1@6
mlpx/1@5 mlp0/1 mlp1/1 means/3@2 mlp2/1 turn1/2@3 mlp3/1 hidden0/2@0 hidden1/2@7 hidden2/2@1 attn/3@6 mlpx/2@4
mlp0/2 hidden3/2@2 mlp1/2 mlp2/2 turn4/0@3 mlp3/2 turn1/3@0 logits/0@5 hidden0/3@7 hidden1/3@1 hidden2/3@2
hidden3/3@6 mlpx/3@3 mlp0/3 mlp1/3 mlp2/3 mlp3/3 turnw/0@7 turn4/1@0 spread0/0@5 spread1/0@4 logits/1@1
spread2/0@2 expert0/0@6 spread3/0@7 expert1/0 spread4/0@0 spread5/0@5 expert2/0 spread6/0@4 spread7/0@1
expert3/0 turn4/2@3 expert4/0 logits/2@2 turnw/1@7 expert5/0 spread0/1@0 expert6/0 spread1/1@3 spread2/1@5
spread3/1@4 spread4/1@7 expert7/0 expert0/1@1 spread5/1@2 spread6/1@0 expert1/1 expert2/1 spread7/1@3 expert3/1
turn4/3@5 expert4/1 logits/3@4 turnw/2@7 expert5/1 expert6/1 spread0/2@2 spread1/2@5 spread2/2@0 expert7/1
spread3/2@3 spread4/2@7 spread5/2@4 expert0/2@2 expert1/2 expert2/2 turnw/3@5 spread6/2@0 expert3/2 expert4/2
spread7/2@3 expert5/2 spread0/3@7 expert6/2 spread1/3@5 spread2/3@4 expert7/2 expert0/3@0 spread3/3@3
spread4/3@7 expert1/3 spread5/3@5 expert2/3 expert3/3 spread6/3@6 spread7/3@4 expert4/3 expert5/3 expert6/3
expert7/3
"""
SCALAR = """
xnT/0 re_abs/0 re_sq/0 im_sq/0 xnT/1 lnm/0 im_sq/1 re_sq/1 mag/0 re_abs/1 lnm/1 log/0 mag/1 k/0 inverse/0 log/1
xnT/2 inverse/1 angle/0 k/1 im_sq/2 decay/0 re_sq/2 angle/1 decay/1 xnT/3 frac_abs/0 sine/0 cosine/0 re_abs/2
frac_abs/1 re_abs/3 cosine/1 sine/1 re_sq/3 gate/0 im_sq/3 lnm/2 k/2 mag/2 lnm/3 im_norm/0 log/2 mag/3 re_norm/0
inverse/2 re_norm/1 cols/0 k/3 log/3 im_norm/1 inverse/3 decay/2 angle/2 y_normed/0 decay/3 angle/3 gate/1
gate/2 frac_abs/2 y_normed/1 sine/2 cosine/2 frac_abs/3 normed1/0 gate/3 sine/3 x1T/0 cosine/3 x1bT/0 gelu0/0
im_norm/2 gelu1/0 re_norm/2 normed1/1 gelu2/0 gelu3/0 x1T/1 x1bT/1 y_normed/2 gelu0/1 gelu1/1 re_norm/3
im_norm/3 normed2/0 gelu2/1 gelu3/1 normed1/2 x1T/2 y_normed/3 x1bT/2 gelu0/2 normed2/1 gelu1/2 gelu2/2
normed4/0 gelu3/2 normed1/3 t4T/0 x1T/3 gelu0/3 x1bT/3 tanh/0 normed2/2 gelu1/3 gelu2/3 gelu3/3 normed4/1 wT/0
t4T/1 tanh/1 normed2/3 normed4/2 t4T/2 wT/1 tanh/2 normed4/3 t4T/3 wT/2 tanh/3 wT/3 normed5/0 normed5/1
normed5/2 last_shift/3
"""
VECTOR = """
stats0/0 moments0/0 stats0/1 moments0/1 normed0/0 stats0/2 moments0/2 stats0/3 normed0/1 mag2/0 moments0/3
normed0/2 mag2/1 den/0 normed0/3 den/1 sign_inv/0 tangent/0 sign_inv/1 kv/0 tangent/1 sum/0 kv/1 mag2/2 frac/0
sum/1 sign_mu/0 sign_mu/1 frac/1 kv_sin/0 kv_cos/0 restart/0 scan_re/0 scan_im/0 q_re/0 kv_sin/1 restart/1
kv_cos/1 q_im/0 scan_re/1 mag2/3 im_sums/0 den/2 y_parts/0 scan_im/1 q_re/1 den/3 q_im/1 means/0 sign_inv/2
im_sums/1 tangent/2 sign_inv/3 y_parts/1 tangent/3 gated/0 sum/2 means/1 sum/3 frac/2 stats1/0 moments1/0 frac/3
gated/1 kv/2 l1b2/0 sign_mu/2 kv_cos/2 restart/2 kv_sin/2 scan_re/2 sign_mu/3 stats1/1 scan_im/2 q_re/2
moments1/1 restart/3 q_im/2 im_sums/2 y_parts/2 kv/3 kv_cos/3 means/2 kv_sin/3 scan_re/3 scan_im/3 q_re/3
stats2/0 gated/2 q_im/3 moments2/0 y_parts/3 stats1/2 moments1/2 im_sums/3 mul2/0 add2/0 means/3 stats3/0
moments3/0 stats2/1 moments2/1 gated/3 x2/0 stats4/0 moments4/0 stats1/3 mul2/1 moments1/3 add2/1 stats3/1
moments3/1 stats2/2 x2/1 moments2/2 route0/0 stats4/1 route1/0 moments4/1 route2/0 route3/0 route4/0 route5/0
route6/0 route7/0 mul2/2 route8/0 add2/2 route9/0 stats3/2 moments3/2 stats2/3 x2/2 weigh0/0 moments2/3 route0/1
weigh1/0 route1/1 stats4/2 route2/1 moments4/2 route3/1 weigh2/0 route4/1 mul2/3 route5/1 weigh3/0 route6/1
weigh4/0 route7/1 add2/3 route8/1 stats3/3 weigh5/0 moments3/3 weigh6/0 route0/2 weigh7/0 route1/2 x2/3 weigh0/1
stats4/3 route2/2 moments4/3 weigh1/1 route3/2 route10/0 weigh2/1 route4/2 route11/0 weigh3/1 weigh4/1 route5/2
route9/1 route6/2 route10/1 route7/2 route8/2 weigh5/1 route11/1 weigh6/1 weigh7/1 route0/3 route1/3 route12/0
route2/3 route13/0 route9/2 route12/1 route3/3 route4/3 route14/0 route5/3 route13/1 weigh0/2 route10/2 route6/3
route14/1 route7/3 route11/2 weigh1/2 route8/3 route12/2 route15/0 weigh2/2 route13/2 route16/0 weigh3/2
route9/3 route14/2 weigh4/2 route15/1 weigh5/2 stats5/0 route16/1 route10/3 route15/2 moments5/0 weigh6/2
route17/0 weigh7/2 stats5/1 route11/3 weigh0/3 route16/2 moments5/1 weigh1/3 route12/3 weigh2/3 route17/1
weigh3/3 stats5/2 route13/3 route17/2 weigh4/3 route14/3 moments5/2 weigh5/3 route15/3 route16/3 weigh6/3
route17/3 weigh7/3 stats5/3 moments5/3 last_sum/3
"""
GPSIMD = """
scale0/0 scale0/1 scale0/2 constants/0 scale0/3 turns/0 whole/0 turns/1 whole/1 y/0 factors/0 turns/2 y/1
turns/3 whole/2 factors/1 whole/3 scale1/0 selectors/0 scale1/1 y/2 factors/2 scale2/0 scale1/2 y/3 factors/3
scale3/0 scale2/1 scale4/0 scale1/3 scale3/1 scale2/2 scale4/1 split/0 scale3/2 scale2/3 scale4/2 split/1
scale3/3 scale4/3 split/2 split/3 scale5/0 out/0 scale5/1 scale5/2 out/1 out/2 scale5/3
"""


def steps_of(table):
    found = []
    for word in table.split():
        word, _, bank = word.partition("@")
        step, _, chunk = word.partition("/")
        found.append((step, int(chunk), int(bank) if bank else None))
    return found


def sandwich(nc, x, Wq, Wk, Wv, Wa, Wg, Wo, gn_scale, gn_bias, ln1_scale, ln1_bias,
             W1, b1, W2, b2, ln2_scale, ln2_bias, router_w, router_b, expert_w, out):
    B, S, D = x.shape
    F = W1.shape[1]
    E = expert_w.shape[0]
    P = 128
    GROUP = D // 32
    NF = F // P
    T = B * S // P
    SEQ = 2
    C = B // SEQ
    N = SEQ * S
    TC = N // P
    PARTS = 3
    NORMS = 6
    EPS = [1e-5, 1e-6, 1e-6, 1e-5, 1e-5, 1e-5]
    EPS_GROUP, EPS_MOE = 1e-6, 1e-10
    ROUND = 1.5 * 2.0 ** 23
    TURN = 2 * math.pi * (1 - 2.0 ** -22)
    TINY = 1e-30
    SIGN = -2 ** 31

    pe_steps, act_steps, dve_steps, pool_steps = [steps_of(t) for t in (TENSOR, SCALAR, VECTOR, GPSIMD)]
    bank_of = {(step, c): b for step, c, b in pe_steps if b is not None}

    ctx = ExitStack()
    with ctx:
        def sb(name, shape, dt=F32):
            return ctx.enter_context(nc.sbuf_tensor(name, shape, dt))

        def sem(name):
            return ctx.enter_context(nc.semaphore(name))

        x_tok = sb("x_tok", [P, T, D])
        xn_tok = sb("xn_tok", [P, T, D])
        n1_tok = sb("n1_tok", [P, T, D])
        a2_tok = sb("a2_tok", [P, T, D])
        x2_tok = sb("x2_tok", [P, T, D])
        t4_tok = sb("t4_tok", [P, T, D])
        xnT = sb("xnT", [P, C, N])
        mu = sb("mu", [P, C, N])
        ang = sb("ang", [P, C, N])
        phase = sb("phase", [P, C, N])
        kv = sb("kv", [P, C, N])
        g_re = sb("g_re", [P, C, N])
        g_im = sb("g_im", [P, C, N])
        y_re = sb("y_re", [P, C, N])
        y_part = sb("y_part", [P, C, N])
        gate = sb("gate", [P, C, N])
        waste = sb("waste", [P, 2, N])
        x1T, x1bT = g_re, g_im
        t4T = phase
        cosT, sinT = ang, phase
        o_tok = y_part
        hid = [kv, mu, ang, gate]
        xs = [kv, mu, ang, gate, xnT, y_re, g_re, g_im]

        wq, wk, wv, wg, wo = [sb(n, [P, D]) for n in ("wq", "wk", "wv", "wg", "wo")]
        wa = sb("wa", [P, 2 * D])
        w1 = sb("w1", [P, F])
        w2 = sb("w2", [P, NF, D])
        we = sb("we", [P, E, D])
        NR = 5 + NF + E
        rows = sb("rows", [NR, D])
        cols = sb("cols", [P, NR])
        gn_s, gn_b, l1_s, l1_b, b2_c = [cols[:, i:i + 1] for i in range(5)]
        b1_c = cols[:, 5:5 + NF]
        rwT = cols[:, 5 + NF:NR]
        l1b2 = sb("l1b2", [P, 1])
        s2_bc = sb("s2_bc", [P, D])
        b2_bc = sb("b2_bc", [P, D])
        rb_row = sb("rb_row", [1, TC * E])
        ones = sb("ones", [1, P])
        ident = sb("ident", [P, P])
        ident_b = sb("ident_b", [P, P], BF16)
        groups = sb("groups", [P, P])
        pick = sb("pick", [PARTS * E, E, P], BF16)
        restart = sb("restart", [P, SEQ, S])
        first_e = sb("first_e", [P, TC, E])
        half_pi = sb("half_pi", [P, 1])
        tiny = sb("tiny", [P, 1])
        power = sb("power", [P, TC])

        bn = sb("bn", [P, NORMS, T, 6])
        mv = sb("mv", [P, NORMS, T, 2])
        veps = sb("veps", [P, NORMS, T])
        rstd = sb("rstd", [P, NORMS, T])
        minus = sb("minus", [P, NORMS, T])
        shift = sb("shift", [P, NORMS, T])
        shift35 = sb("shift35", [P, T])
        epsf = sb("epsf", [P, T])
        gst = sb("gst", [P, C, 2, 3, SEQ])
        gmean = sb("gmean", [P, C, 3, SEQ])
        gvar = sb("gvar", [P, C, SEQ])
        gw = sb("gw", [P, C, 4, SEQ])
        gn_a = sb("gn_a", [P, C, SEQ])
        gn_c = sb("gn_c", [P, C, SEQ])
        ro = sb("ro", [P, C, 12, TC, E])
        r4 = sb("r4", [P, C, 12, TC])
        wsp = sb("wsp", [P, C, TC, PARTS, E], BF16)
        wrest = sb("wrest", [P, C, 2, TC, E])
        wT = sb("wT", [PARTS * E, C, N], BF16)

        ps = ctx.enter_context(nc.psum_tensor("ps", [P, 8, N], F32))

        def bank(step, c):
            return ps[:, bank_of[step, c], :]

        def tiles(b):
            return b.rearrange("p (t d) -> p t d", d=D)

        def tl(c):
            return slice(TC * c, TC * (c + 1))

        def tok(k):
            return slice(P * k, P * (k + 1))

        s_x = [sem(f"x_loaded{c}") for c in range(C)]
        s_wa = sem("wa_loaded")
        s_rows = sem("rows_loaded")
        s_wkv = sem("kv_gq_weights_loaded")
        s_wmlp = sem("mlp_weights_loaded")
        s_wmoe = sem("moe_weights_loaded")
        s_bc = sem("broadcasts_loaded")
        s_out = sem("out_stored")
        ident_ok = sem("identity_made")
        consts = sem("consts_made")
        warmed = sem("array_warmed")
        colsT = sem("cols_in_psum")
        cols_ok = sem("cols_made")
        l1b2_ok = sem("l1b2_made")
        bn_ok = [sem(f"stats{n}_made") for n in range(NORMS)]
        mv_ok = [sem(f"moments{n}_made") for n in range(NORMS)]
        ve_ok = [sem(f"var_eps{n}_made") for n in range(NORMS)]
        rs_ok = [sem(f"rstd{n}_made") for n in range(NORMS)]
        sh_ok = [sem(f"shift{n}_made") for n in range(NORMS)]
        sh35_ok = sem("shift35_made")
        xn_ok = sem("xn_made")
        xnT_ps = sem("xnT_in_psum")
        xnT_ok = sem("xnT_made")
        ar_ps = sem("re_a_in_psum")
        ai_ps = sem("im_a_in_psum")
        sqr_ok = sem("re_square_made")
        sqi_ok = sem("im_square_made")
        absre_ok = sem("abs_re_made")
        mag2_ok = sem("mag2_made")
        lnm_ok = sem("log_mag2_made")
        mag_ok = sem("mag_made")
        den_ok = sem("den_made")
        ln_ok = sem("log_made")
        inv_ok = sem("inverse_made")
        sinv_ok = sem("signed_inverse_made")
        tan_ok = sem("tangent_made")
        sig_ok = sem("sigmoid_made")
        ang_ok = sem("angle_made")
        smu_ok = sem("signed_decay_made")
        mu_ok = sem("decay_restarts_made")
        turn_ok = sem("turns_made")
        sum_ok = sem("phase_summed")
        whole_ok = sem("whole_turns_made")
        frac_ok = sem("phase_wrapped")
        k_ps = sem("k_in_psum")
        v_ps = sem("v_in_psum")
        k_ok = sem("k_copied")
        kv_ok = sem("kv_made")
        g_ps = sem("g_in_psum")
        q_ps = sem("q_in_psum")
        sin_ok = sem("sine_made")
        abs_ok = sem("abs_phase_made")
        cos_ok = sem("cosine_made")
        gate_ok = sem("gate_made")
        kc_ok = sem("kv_cos_made")
        ks_ok = sem("kv_sin_made")
        scr_ok = sem("re_scanned")
        sci_ok = sem("im_scanned")
        qr_ok = sem("q_times_re")
        qi_ok = sem("q_times_im")
        pr_ok = sem("y_parts_made")
        pi_ok = sem("im_sums_made")
        nr_ok = sem("re_square_sums_made")
        ni_ok = sem("im_square_sums_made")
        y_ok = sem("y_made")
        gm_ps = sem("group_means_in_psum")
        gm_ok = sem("group_means_made")
        mk = sem("constant_steps")
        gp = sem("group_norm_steps")
        vs = sem("group_variance_steps")
        gn_ok = sem("group_norm_factors_made")
        yn_ok = sem("y_normed")
        z_ok = sem("y_gated")
        o_ps = sem("attention_out_in_psum")
        n1_ok = sem("n1_made")
        n1T_ps = sem("n1T_in_psum")
        x1T_ok = sem("x1T_made")
        x1b_ok = sem("x1bT_made")
        h_ps = sem("hidden_in_psum")
        h_ok = sem("hidden_made")
        m_ps = sem("mlp_out_in_psum")
        n2_ok = sem("n2_made")
        u2_ok = sem("n2_scaled")
        a2_ok = sem("a2_made")
        x2_ok = sem("x2_made")
        t4_ok = sem("t4_made")
        t4T_ps = sem("t4T_in_psum")
        t4T_ok = sem("t4T_made")
        lg_ps = sem("logits_in_psum")
        rt = [sem(f"route{n}_done") for n in range(17)]
        th_ok = sem("tanh_made")
        epsf_ok = sem("eps_over_factor_square_made")
        sp = sem("split_steps")
        wsp_ok = sem("token_weights_split")
        wT_ps = sem("wT_in_psum")
        wT_ok = sem("wT_made")
        wb_ps = sem("weights_spread")
        xs_ok = sem("tokens_weighted")
        e_ps = sem("experts_in_psum")
        o_ok = sem("experts_normed")
        last_ok = sem("last_sums_made")
        out_ok = [sem(f"out{c}_made") for c in range(C)]

        block = ctx.enter_context(nc.Block())

        @block.sync
        def _(sync):
            xt = x.rearrange("b s d -> (b s) d").rearrange("(t p) d -> p t d", p=P)
            ot = out.rearrange("b s d -> (b s) d").rearrange("(t p) d -> p t d", p=P)
            for c in range(C):
                sync.dma_start(x_tok[:, tl(c), :], xt[:, tl(c), :]).then_inc(s_x[c], 16)
                if c == 0:
                    sync.dma_start(wa[:, :], Wa).then_inc(s_wa, 16)
                elif c == 1:
                    sync.dma_start(wk[:, :], Wk).then_inc(s_wkv, 16)
                    sync.dma_start(wv[:, :], Wv).then_inc(s_wkv, 16)
                elif c == 2:
                    sync.dma_start(wg[:, :], Wg).then_inc(s_wkv, 16)
                    sync.dma_start(wq[:, :], Wq).then_inc(s_wkv, 16)
            for i, v in enumerate((gn_scale, gn_bias, ln1_scale, ln1_bias, b2)):
                sync.dma_start(rows[i:i + 1, :], v.rearrange("(a d) -> a d", a=1)).then_inc(s_rows, 16)
            sync.dma_start(rows[5:5 + NF, :], b1.rearrange("(f d) -> f d", d=P)).then_inc(s_rows, 16)
            sync.dma_start(rows[5 + NF:NR, :], router_w).then_inc(s_rows, 16)
            sync.dma_start(wo[:, :], Wo).then_inc(s_wmlp, 16)
            sync.dma_start(w1[:, :], W1).then_inc(s_wmlp, 16)
            sync.dma_start(w2[:, :, :], W2.rearrange("(f p) d -> p f d", p=P)).then_inc(s_wmlp, 16)
            sync.dma_start(we[:, :, :], expert_w.rearrange("e h d -> h e d")).then_inc(s_wmoe, 16)
            sync.dma_start(s2_bc[:, :], ln2_scale.partition_broadcast(P)).then_inc(s_bc, 16)
            sync.dma_start(b2_bc[:, :], ln2_bias.partition_broadcast(P)).then_inc(s_bc, 16)
            sync.dma_start(rb_row[:, :].rearrange("p (t e) -> p t e", e=E),
                           router_b.rearrange("(a b e) -> a b e", a=1, b=1).to_broadcast([1, TC, E])).then_inc(s_bc, 16)
            for c in range(C - 1):
                sync.wait_ge(out_ok[c], 1)
                sync.dma_start(ot[:, tl(c), :], tiles(o_tok[:, c, :])).then_inc(s_out, 16)
            for h in range(2):
                half = slice(TC // 2 * h, TC // 2 * (h + 1))
                sync.wait_ge(out_ok[C - 1], TC // 2 * (h + 1))
                sync.dma_start(ot[:, tl(C - 1), :][:, half, :], tiles(o_tok[:, C - 1, :])[:, half, :]).then_inc(s_out, 16)
            sync.wait_ge(s_out, 16 * (C + 1))

        @block.gpsimd
        def _(pool):
            pool.memset(ident[:, :], 0.0).then_inc(mk, 1)
            pool.memset(power[:, :], -0.5)
            pool.memset(tiny[:, :], TINY)
            pool.wait_ge(mk, 1)
            pool.affine_select(out=ident[:, :], in_=ident[:, :], compare_op=ALU.not_equal, fill=1.0,
                               base=0, pattern=[[-1, P]], channel_multiplier=1).then_inc(ident_ok, 1)

            for step, c, _ in pool_steps:
                if step == "constants":
                    pool.memset(restart[:, :, :], 1.0).then_inc(mk, 1)
                    pool.memset(groups[:, :], 1.0 / (GROUP * S)).then_inc(mk, 1)
                    pool.memset(pick[:, :, :], 0.0).then_inc(mk, 1)
                    pool.memset(first_e[:, :, :], 1.0).then_inc(mk, 1)
                    pool.memset(half_pi[:, :], math.pi / 2)
                    pool.memset(ones[:, :], 1.0)
                    pool.wait_ge(mk, 5)
                    pool.memset(first_e[:, :, 0:1], 0.0)
                    pool.memset(restart[:, :, 0:1], 0.0).then_inc(consts, 1)
                    gv = groups[:, :].rearrange("p (g j) -> p g j", j=GROUP)
                    pool.affine_select(out=gv, in_=gv, compare_op=ALU.is_ge, fill=0.0, base=0,
                                       pattern=[[-GROUP, D // GROUP], [0, GROUP]],
                                       channel_multiplier=1).then_inc(mk, 1)
                    pool.wait_ge(mk, 6)
                    pool.affine_select(out=gv, in_=gv, compare_op=ALU.is_ge, fill=0.0, base=GROUP - 1,
                                       pattern=[[GROUP, D // GROUP], [0, GROUP]],
                                       channel_multiplier=-1).then_inc(consts, 1)
                elif step == "selectors":
                    for n in range(PARTS):
                        pool.affine_select(out=pick[:, :, :], in_=pick[:, :, :], compare_op=ALU.not_equal,
                                           fill=1.0, base=-E * n, pattern=[[-1, E], [0, P]],
                                           channel_multiplier=1).then_inc(mk, 1)
                        pool.wait_ge(mk, 7 + n)
                    pool.tensor_copy(ident_b[:, :], ident[:, :]).then_inc(consts, 1)
                elif step.startswith("scale"):
                    n = int(step[5:])
                    pool.wait_ge(mv_ok[n], c + 1)
                    if n < 5:
                        pool.tensor_scalar(veps[:, n, tl(c)], mv[:, n, tl(c), 1], 1.0, EPS[n],
                                           ALU.mult, ALU.add).then_inc(ve_ok[n], 1)
                    else:
                        pool.wait_ge(epsf_ok, c + 1)
                        pool.tensor_tensor(veps[:, n, tl(c)], mv[:, n, tl(c), 1], epsf[:, tl(c)],
                                           ALU.add).then_inc(ve_ok[n], 1)
                    if n > 0:
                        pool.tensor_scalar(minus[:, n, tl(c)], mv[:, n, tl(c), 0], -1.0, 0.0, ALU.mult, ALU.add)
                    pool.wait_ge(ve_ok[n], c + 1)
                    pool.tensor_tensor(rstd[:, n, tl(c)], veps[:, n, tl(c)], power[:, :],
                                       ALU.pow).then_inc(rs_ok[n], 1)
                    if n > 0:
                        pool.wait_ge(rs_ok[n], c + 1)
                        pool.tensor_tensor(shift[:, n, tl(c)], minus[:, n, tl(c)], rstd[:, n, tl(c)],
                                           ALU.mult).then_inc(sh_ok[n], 1)
                    if n == 5:
                        pool.wait_ge(sh_ok[5], c + 1)
                        pool.tensor_tensor(shift35[:, tl(c)], shift[:, 3, tl(c)], shift[:, 5, tl(c)],
                                           ALU.add).then_inc(sh35_ok, 1)
                elif step == "turns":
                    pool.wait_ge(ang_ok, c + 1)
                    pool.tensor_scalar(ang[:, c, :], ang[:, c, :], 1.0 / math.pi, 0.0,
                                       ALU.mult, ALU.add).then_inc(turn_ok, 1)
                elif step == "whole":
                    pool.wait_ge(sum_ok, c + 1)
                    pool.tensor_scalar(ang[:, c, :], phase[:, c, :], 1.0, ROUND, ALU.mult, ALU.add).then_inc(whole_ok, 1)
                elif step == "factors":
                    pool.wait_ge(cols_ok, 1)
                    pool.wait_ge(gm_ok, c + 1)
                    m, w = gmean[:, c], gw[:, c]
                    pool.tensor_tensor(w[:, 2, :], gvar[:, c, :], power[:, 0:SEQ], ALU.pow).then_inc(gp, 1)
                    pool.wait_ge(gp, 3 * c + 1)
                    pool.tensor_tensor(gn_a[:, c, :], w[:, 2, :], gn_s.to_broadcast([P, SEQ]), ALU.mult).then_inc(gp, 1)
                    pool.wait_ge(gp, 3 * c + 2)
                    pool.tensor_tensor(w[:, 3, :], m[:, 0, :], gn_a[:, c, :], ALU.mult).then_inc(gp, 1)
                    pool.wait_ge(gp, 3 * c + 3)
                    pool.tensor_tensor(gn_c[:, c, :], gn_b.to_broadcast([P, SEQ]), w[:, 3, :],
                                       ALU.subtract).then_inc(gn_ok, 1)
                elif step == "y":
                    pool.wait_ge(pr_ok, 2 * SEQ * (c + 1))
                    pool.tensor_tensor(y_re[:, c, :], y_re[:, c, :], y_part[:, c, :], ALU.add).then_inc(y_ok, 1)
                elif step == "out":
                    pool.wait_ge(o_ok, c + 1)
                    pool.tensor_tensor(tiles(o_tok[:, c, :]), tiles(o_tok[:, c, :]), x2_tok[:, tl(c), :],
                                       ALU.add).then_inc(out_ok[c], 1)
                elif step == "split":
                    pool.wait_ge(rt[8], c + 1)
                    rest = ro[:, c, 9]
                    for n in range(PARTS - 1):
                        pool.tensor_copy(wsp[:, c, :, n, :], rest).then_inc(sp, 1)
                        pool.wait_ge(sp, 2 * (PARTS - 1) * c + 2 * n + 1)
                        pool.tensor_tensor(wrest[:, c, n], rest, wsp[:, c, :, n, :], ALU.subtract).then_inc(sp, 1)
                        pool.wait_ge(sp, 2 * (PARTS - 1) * c + 2 * n + 2)
                        rest = wrest[:, c, n]
                    pool.tensor_copy(wsp[:, c, :, PARTS - 1, :], rest).then_inc(wsp_ok, 1)

        @block.tensor
        def _(pe):
            def reader(step, c):
                one = {"cols": cols_ok, "turn0": xnT_ok, "re_a": smu_ok, "im_a": tan_ok, "k": k_ok, "v": kv_ok,
                       "g": gate_ok, "q": qi_ok, "means": gm_ok, "attn": n1_ok, "warm": warmed, "turn1": x1b_ok, "mlpx": n2_ok,
                       "turn4": t4T_ok, "logits": rt[1], "turnw": wT_ok, "expert0": o_ok}
                if step in one:
                    return one[step], c + 1
                kind, n = step[:-1], int(step[-1])
                return (h_ok, NF * c + n + 1) if kind == "hidden" else (xs_ok, E * c + n + 1)

            held = {}

            def turn(b, src, c, done):
                for k in range(TC):
                    ins = pe.transpose(b[:, tok(k)], src[:, TC * c + k, :], ident[:, :])
                ins.then_inc(done, 1)

            for step, c, b in pe_steps:
                if b is not None:
                    if b in held:
                        pe.wait_ge(*reader(*held[b]))
                    held[b] = (step, c)
                if step == "warm":
                    pe.wait_ge(ident_ok, 1)
                    for k in range(30):
                        ins = pe.transpose(bank("warm", 0)[:, 0:P], ident[:, :], ident[:, :])
                    ins.then_inc(warmed, 1)
                elif step == "cols":
                    pe.wait_ge(s_rows, 16 * 7)
                    pe.wait_ge(ident_ok, 1)
                    pe.transpose(bank("cols", 0)[:, 0:NR], rows[:, :], ident[0:NR, 0:NR]).then_inc(colsT, 1)
                elif step == "turn0":
                    pe.wait_ge(ident_ok, 1)
                    pe.wait_ge(xn_ok, c + 1)
                    turn(bank("turn0", c), xn_tok, c, xnT_ps)
                elif step == "re_a":
                    pe.wait_ge(s_wa, 16)
                    pe.wait_ge(xnT_ok, c + 1)
                    pe.matmul(bank("re_a", c), wa[:, 0:D], xnT[:, c, :], start=True, stop=True).then_inc(ar_ps, 1)
                elif step == "im_a":
                    pe.wait_ge(xnT_ok, c + 1)
                    pe.matmul(bank("im_a", c), wa[:, D:2 * D], xnT[:, c, :], start=True, stop=True).then_inc(ai_ps, 1)
                elif step in ("k", "v", "g", "q"):
                    w, done = {"k": (wk, k_ps), "v": (wv, v_ps), "g": (wg, g_ps), "q": (wq, q_ps)}[step]
                    pe.wait_ge(s_wkv, 16 * 4)
                    pe.wait_ge(xnT_ok, c + 1)
                    pe.matmul(bank(step, c), w[:, :], xnT[:, c, :], start=True, stop=True).then_inc(done, 1)
                elif step == "means":
                    pe.wait_ge(consts, 2)
                    pe.wait_ge(pr_ok, 2 * SEQ * (c + 1))
                    pe.wait_ge(pi_ok, 2 * SEQ * (c + 1))
                    pe.wait_ge(nr_ok, SEQ * (c + 1))
                    pe.wait_ge(ni_ok, SEQ * (c + 1))
                    for n in range(2):
                        ins = pe.matmul(bank("means", c)[:, 0:3 * SEQ], groups[:, :],
                                        gst[:, c, n].rearrange("p k s -> p (k s)"), start=(n == 0), stop=(n == 1))
                    ins.then_inc(gm_ps, 1)
                elif step == "attn":
                    pe.wait_ge(s_wmlp, 16 * 3)
                    pe.wait_ge(z_ok, c + 1)
                    for k in range(TC):
                        pe.matmul(bank("attn", c)[:, tok(k)], xnT[:, c, tok(k)], ident[:, :], start=True, stop=False)
                        ins = pe.matmul(bank("attn", c)[:, tok(k)], y_re[:, c, tok(k)], wo[:, :],
                                        start=False, stop=True)
                    ins.then_inc(o_ps, 1)
                elif step == "turn1":
                    pe.wait_ge(n1_ok, c + 1)
                    turn(bank("turn1", c), n1_tok, c, n1T_ps)
                elif step.startswith("hidden"):
                    f = int(step[-1])
                    pe.wait_ge(x1T_ok, c + 1)
                    pe.matmul(bank(step, c), w1[:, P * f:P * (f + 1)], x1T[:, c, :],
                              start=True, stop=True).then_inc(h_ps, 1)
                elif step == "mlpx":
                    pe.wait_ge(x1b_ok, c + 1)
                    for k in range(TC):
                        pe.matmul(bank("mlpx", c)[:, tok(k)], x1bT[:, c, tok(k)], ident[:, :],
                                  start=(k == 0), stop=False, skip_group_check=True)
                elif step.startswith("mlp"):
                    f = int(step[-1])
                    pe.wait_ge(h_ok, NF * c + f + 1)
                    for k in range(TC):
                        ins = pe.matmul(bank("mlpx", c)[:, tok(k)], hid[f][:, c, tok(k)], w2[:, f, :],
                                        start=False, stop=(f == NF - 1), skip_group_check=True)
                    if f == NF - 1:
                        ins.then_inc(m_ps, 1)
                elif step == "turn4":
                    pe.wait_ge(t4_ok, c + 1)
                    turn(bank("turn4", c), t4_tok, c, t4T_ps)
                elif step == "logits":
                    pe.wait_ge(t4T_ok, c + 1)
                    pe.wait_ge(consts, 1)
                    pe.wait_ge(s_bc, 16 * 3)
                    pe.matmul(bank("logits", c)[:, 0:TC * E], ones[:, :], rb_row[:, :], start=True, stop=False,
                              skip_group_check=True)
                    for k in range(TC):
                        ins = pe.matmul(bank("logits", c)[:, E * k:E * (k + 1)], t4T[:, c, tok(k)], rwT,
                                        start=False, stop=True, skip_group_check=True)
                    ins.then_inc(lg_ps, 1)
                elif step == "turnw":
                    pe.wait_ge(consts, 3)
                    pe.wait_ge(wsp_ok, c + 1)
                    for k in range(TC):
                        ins = pe.transpose(bank("turnw", c).bitcast(BF16)[0:PARTS * E, tok(k)],
                                           wsp[:, c, k].rearrange("p n e -> p (n e)"), ident_b[:, :])
                    ins.then_inc(wT_ps, 1)
                elif step.startswith("spread"):
                    e = int(step[-1])
                    pe.wait_ge(wT_ok, c + 1)
                    pe.matmul(bank(step, c), pick[:, e, :], wT[:, c, :], start=True, stop=True).then_inc(wb_ps, 1)
                elif step.startswith("expert"):
                    e = int(step[-1])
                    pe.wait_ge(s_wmoe, 16)
                    pe.wait_ge(xs_ok, E * c + e + 1)
                    for k in range(TC):
                        ins = pe.matmul(bank("expert0", c)[:, tok(k)], xs[e][:, c, tok(k)], we[:, e, :],
                                        start=(e == 0 and k == 0), stop=(e == E - 1), skip_group_check=True)
                    if e == E - 1:
                        ins.then_inc(e_ps, 1)

        @block.scalar
        def _(act):
            tables = {"lnm": "natural_log_exp_and_others", "mag": "natural_log_exp_and_others",
                      "log": "natural_log_exp_and_others",
                      "inverse": "natural_log_exp_and_others", "decay": "sigmoid_and_others",
                      "angle": "sigmoid_and_others", "gate": "silu_and_others", "cosine": "silu_and_others",
                      "sine": "silu_and_others", "tanh": "gelu_apprx_tanh_and_others"}
            tables |= {f"gelu{f}": "gelu_apprx_tanh_and_others" for f in range(NF)}
            loaded = "natural_log_exp_and_others"
            act.preload_act_table_set(loaded)

            def normed(n, c, dst, tile_of, done):
                act.wait_ge(sh_ok[n], c + 1)
                for k in range(TC):
                    t = TC * c + k
                    ins = act.activation(dst[:, t, :], tile_of(k), ACT.Identity,
                                         scale=rstd[:, n, t:t + 1], bias=shift[:, n, t:t + 1])
                ins.then_inc(done, 1)

            for step, c, _ in act_steps:
                if tables.get(step, loaded) != loaded:
                    loaded = tables[step]
                    act.preload_act_table_set(loaded)
                if step == "cols":
                    act.wait_ge(colsT, 1)
                    act.activation(cols[:, :], bank("cols", 0)[:, 0:NR], ACT.Copy).then_inc(cols_ok, 1)
                elif step == "xnT":
                    act.wait_ge(xnT_ps, c + 1)
                    act.activation(xnT[:, c, :], bank("turn0", c), ACT.Copy).then_inc(xnT_ok, 1)
                elif step == "re_sq":
                    act.wait_ge(ar_ps, c + 1)
                    act.activation(mu[:, c, :], bank("re_a", c), ACT.Square).then_inc(sqr_ok, 1)
                elif step == "im_sq":
                    act.wait_ge(ai_ps, c + 1)
                    act.activation(ang[:, c, :], bank("im_a", c), ACT.Square).then_inc(sqi_ok, 1)
                elif step == "re_abs":
                    act.wait_ge(ar_ps, c + 1)
                    act.activation(y_part[:, c, :], bank("re_a", c), ACT.Abs).then_inc(absre_ok, 1)
                elif step == "lnm":
                    act.wait_ge(mag2_ok, c + 1)
                    act.wait_ge(ident_ok, 1)
                    act.activation(mu[:, c, :], mu[:, c, :], ACT.Ln, bias=tiny[:, :]).then_inc(lnm_ok, 1)
                elif step == "mag":
                    act.wait_ge(lnm_ok, c + 1)
                    act.activation(mu[:, c, :], mu[:, c, :], ACT.Exp, scale=0.5).then_inc(mag_ok, 1)
                elif step == "log":
                    act.wait_ge(den_ok, c + 1)
                    act.activation(ang[:, c, :], ang[:, c, :], ACT.Ln).then_inc(ln_ok, 1)
                elif step == "inverse":
                    act.wait_ge(ln_ok, c + 1)
                    act.activation(ang[:, c, :], ang[:, c, :], ACT.Exp, scale=-1.0).then_inc(inv_ok, 1)
                elif step == "decay":
                    act.wait_ge(den_ok, c + 1)
                    act.activation(mu[:, c, :], mu[:, c, :], ACT.Sigmoid).then_inc(sig_ok, 1)
                elif step == "angle":
                    act.wait_ge(tan_ok, c + 1)
                    act.activation(ang[:, c, :], ang[:, c, :], ACT.Arctan).then_inc(ang_ok, 1)
                elif step == "k":
                    act.wait_ge(k_ps, c + 1)
                    act.activation(kv[:, c, :], bank("k", c), ACT.Copy).then_inc(k_ok, 1)
                elif step == "gate":
                    act.wait_ge(g_ps, c + 1)
                    act.activation(gate[:, c, :], bank("g", c), ACT.Silu).then_inc(gate_ok, 1)
                elif step == "frac_abs":
                    act.wait_ge(frac_ok, c + 1)
                    act.activation(cosT[:, c, :], phase[:, c, :], ACT.Abs).then_inc(abs_ok, 1)
                elif step == "cosine":
                    act.wait_ge(abs_ok, c + 1)
                    act.activation(cosT[:, c, :], cosT[:, c, :], ACT.Sin, scale=-TURN,
                                   bias=half_pi[:, :]).then_inc(cos_ok, 1)
                elif step == "sine":
                    act.wait_ge(abs_ok, c + 1)
                    act.activation(sinT[:, c, :], phase[:, c, :], ACT.Sin, scale=-TURN).then_inc(sin_ok, 1)
                elif step in ("re_norm", "im_norm"):
                    n, g, ready, done = (0, g_re, qr_ok, nr_ok) if step == "re_norm" else (1, g_im, qi_ok, ni_ok)
                    act.wait_ge(ready, c + 1)
                    if c >= 1:
                        act.wait_ge(done, SEQ * c)
                    for s in range(SEQ):
                        t = slice(s * S, (s + 1) * S)
                        act.activation(waste[:, n, t], g[:, c, t], ACT.Square,
                                       accum_out=gst[:, c, n, 2, s:s + 1]).then_inc(done, 1)
                elif step == "y_normed":
                    act.wait_ge(gn_ok, c + 1)
                    act.wait_ge(y_ok, c + 1)
                    for s in range(SEQ):
                        t = slice(s * S, (s + 1) * S)
                        ins = act.activation(y_re[:, c, t], y_re[:, c, t], ACT.Identity,
                                             scale=gn_a[:, c, s:s + 1], bias=gn_c[:, c, s:s + 1])
                    ins.then_inc(yn_ok, 1)
                elif step == "normed1":
                    normed(1, c, n1_tok, lambda k: bank("attn", c)[:, tok(k)], n1_ok)
                elif step == "x1T":
                    act.wait_ge(n1T_ps, c + 1)
                    act.wait_ge(cols_ok, 1)
                    act.activation(x1T[:, c, :], bank("turn1", c), ACT.Identity, scale=l1_s, bias=l1_b).then_inc(x1T_ok, 1)
                elif step == "x1bT":
                    act.wait_ge(l1b2_ok, 1)
                    act.wait_ge(n1T_ps, c + 1)
                    act.activation(x1bT[:, c, :], bank("turn1", c), ACT.Identity, scale=l1_s,
                                   bias=l1b2[:, :]).then_inc(x1b_ok, 1)
                elif step.startswith("gelu"):
                    f = int(step[-1])
                    act.wait_ge(h_ps, NF * c + f + 1)
                    act.activation(hid[f][:, c, :], bank(f"hidden{f}", c), ACT.Gelu_apprx_tanh,
                                   bias=b1_c[:, f:f + 1]).then_inc(h_ok, 1)
                elif step == "normed2":
                    normed(2, c, a2_tok, lambda k: bank("mlpx", c)[:, tok(k)], n2_ok)
                elif step == "normed4":
                    act.wait_ge(x2_ok, c + 1)
                    normed(4, c, t4_tok, lambda k: x2_tok[:, TC * c + k, :], t4_ok)
                elif step == "t4T":
                    act.wait_ge(t4T_ps, c + 1)
                    act.activation(t4T[:, c, :], bank("turn4", c), ACT.Copy).then_inc(t4T_ok, 1)
                elif step == "tanh":
                    act.wait_ge(rt[1], c + 1)
                    act.activation(ro[:, c, 1], ro[:, c, 0], ACT.Tanh, scale=0.5).then_inc(th_ok, 1)
                elif step == "wT":
                    act.wait_ge(wT_ps, c + 1)
                    act.activation(wT[:, c, :], bank("turnw", c).bitcast(BF16)[0:PARTS * E, 0:N],
                                   ACT.Copy).then_inc(wT_ok, 1)
                elif step == "last_shift":
                    act.wait_ge(sh35_ok, c + 1)
                    for k in range(TC):
                        t = TC * c + k
                        act.wait_ge(last_ok, k + 1)
                        act.activation(tiles(o_tok[:, c, :])[:, k, :], tiles(o_tok[:, c, :])[:, k, :], ACT.Identity,
                                       bias=shift35[:, t:t + 1]).then_inc(out_ok[c], 1)
                elif step == "normed5":
                    act.wait_ge(sh35_ok, c + 1)
                    for k in range(TC):
                        t = TC * c + k
                        ins = act.activation(tiles(o_tok[:, c, :])[:, k, :], bank("expert0", c)[:, tok(k)],
                                             ACT.Identity, scale=rstd[:, 5, t:t + 1], bias=shift35[:, t:t + 1])
                    ins.then_inc(o_ok, 1)

        @block.vector
        def _(dve):
            def over_e(v):
                return v.unsqueeze(2).to_broadcast([P, TC, E])

            def stats(n, c, ready, count, tile_of):
                dve.wait_ge(ready, count)
                for k in range(TC):
                    ins = dve.bn_stats(bn[:, n, TC * c + k, :], tile_of(k))
                ins.then_inc(bn_ok[n], 1)

            for step, c, _ in dve_steps:
                if step == "l1b2":
                    dve.wait_ge(cols_ok, 1)
                    dve.tensor_tensor(l1b2[:, :], l1_b, b2_c, ALU.add).then_inc(l1b2_ok, 1)
                elif step == "stats0":
                    stats(0, c, s_x[c], 16, lambda k: x_tok[:, TC * c + k, :])
                elif step == "stats1":
                    stats(1, c, o_ps, c + 1, lambda k: bank("attn", c)[:, tok(k)])
                elif step == "stats2":
                    stats(2, c, m_ps, c + 1, lambda k: bank("mlpx", c)[:, tok(k)])
                elif step == "stats3":
                    stats(3, c, a2_ok, c + 1, lambda k: a2_tok[:, TC * c + k, :])
                elif step == "stats4":
                    stats(4, c, x2_ok, c + 1, lambda k: x2_tok[:, TC * c + k, :])
                elif step == "stats5":
                    stats(5, c, e_ps, c + 1, lambda k: bank("expert0", c)[:, tok(k)])
                elif step.startswith("moments"):
                    n = int(step[-1])
                    dve.wait_ge(bn_ok[n], c + 1)
                    for k in range(TC):
                        ins = dve.bn_aggr(mv[:, n, TC * c + k, :], bn[:, n, TC * c + k, :])
                    ins.then_inc(mv_ok[n], 1)
                elif step == "normed0":
                    dve.wait_ge(rs_ok[0], c + 1)
                    for k in range(TC):
                        t = TC * c + k
                        ins = dve.tensor_scalar(xn_tok[:, t, :], x_tok[:, t, :], mv[:, 0, t, 0:1], rstd[:, 0, t:t + 1],
                                                ALU.subtract, ALU.mult)
                    ins.then_inc(xn_ok, 1)
                elif step == "mag2":
                    dve.wait_ge(sqr_ok, c + 1)
                    dve.wait_ge(sqi_ok, c + 1)
                    dve.tensor_tensor(mu[:, c, :], mu[:, c, :], ang[:, c, :], ALU.add).then_inc(mag2_ok, 1)
                elif step == "den":
                    dve.wait_ge(mag_ok, c + 1)
                    dve.wait_ge(absre_ok, c + 1)
                    dve.tensor_tensor(ang[:, c, :], y_part[:, c, :], mu[:, c, :], ALU.add).then_inc(den_ok, 1)
                elif step == "sign_inv":
                    dve.wait_ge(inv_ok, c + 1)
                    dve.scalar_tensor_tensor(out=ang[:, c, :].bitcast(I32), in0=bank("re_a", c).bitcast(I32),
                                             scalar=SIGN, in1=ang[:, c, :].bitcast(I32),
                                             op0=ALU.bitwise_and, op1=ALU.bitwise_or).then_inc(sinv_ok, 1)
                elif step == "tangent":
                    dve.wait_ge(sinv_ok, c + 1)
                    dve.tensor_tensor(ang[:, c, :], bank("im_a", c), ang[:, c, :], ALU.mult).then_inc(tan_ok, 1)
                elif step == "sign_mu":
                    dve.wait_ge(sig_ok, c + 1)
                    dve.scalar_tensor_tensor(out=mu[:, c, :].bitcast(I32), in0=bank("re_a", c).bitcast(I32),
                                             scalar=SIGN, in1=mu[:, c, :].bitcast(I32),
                                             op0=ALU.bitwise_and, op1=ALU.bitwise_or).then_inc(smu_ok, 1)
                elif step == "restart":
                    dve.wait_ge(smu_ok, c + 1)
                    dve.memset(mu[:, c, :].rearrange("p (s t) -> p s t", t=S)[:, :, 0:1], 0.0).then_inc(mu_ok, 1)
                elif step == "sum":
                    dve.wait_ge(consts, 1)
                    dve.wait_ge(turn_ok, c + 1)
                    dve.tensor_tensor_scan(phase[:, c, :], restart[:, :, :].rearrange("p s t -> p (s t)"),
                                           ang[:, c, :], 0.0, ALU.mult, ALU.add).then_inc(sum_ok, 1)
                elif step == "frac":
                    dve.wait_ge(whole_ok, c + 1)
                    dve.scalar_tensor_tensor(out=phase[:, c, :], in0=ang[:, c, :], scalar=ROUND,
                                             in1=phase[:, c, :], op0=ALU.subtract,
                                             op1=ALU.subtract).then_inc(frac_ok, 1)
                elif step == "kv":
                    dve.wait_ge(v_ps, c + 1)
                    dve.wait_ge(k_ok, c + 1)
                    dve.tensor_tensor(kv[:, c, :], bank("v", c), kv[:, c, :], ALU.mult).then_inc(kv_ok, 1)
                elif step == "kv_cos":
                    dve.wait_ge(kv_ok, c + 1)
                    dve.wait_ge(cos_ok, c + 1)
                    dve.tensor_tensor(g_re[:, c, :], kv[:, c, :], cosT[:, c, :], ALU.mult).then_inc(kc_ok, 1)
                elif step == "kv_sin":
                    dve.wait_ge(kv_ok, c + 1)
                    dve.wait_ge(sin_ok, c + 1)
                    dve.tensor_tensor(g_im[:, c, :], kv[:, c, :], sinT[:, c, :], ALU.mult).then_inc(ks_ok, 1)
                elif step in ("scan_re", "scan_im"):
                    g, ready, done = (g_re, kc_ok, scr_ok) if step == "scan_re" else (g_im, ks_ok, sci_ok)
                    dve.wait_ge(mu_ok, c + 1)
                    dve.wait_ge(ready, c + 1)
                    dve.tensor_tensor_scan(g[:, c, :], mu[:, c, :], g[:, c, :], 0.0,
                                           ALU.mult, ALU.add).then_inc(done, 1)
                elif step in ("q_re", "q_im"):
                    g, ready, done = (g_re, scr_ok, qr_ok) if step == "q_re" else (g_im, sci_ok, qi_ok)
                    dve.wait_ge(q_ps, c + 1)
                    dve.wait_ge(ready, c + 1)
                    dve.tensor_tensor(g[:, c, :], bank("q", c), g[:, c, :], ALU.mult).then_inc(done, 1)
                elif step in ("y_parts", "im_sums"):
                    if step == "y_parts":
                        todo, part, done = ((y_re, g_re, cosT, 1.0), (y_part, g_im, sinT, 1.0)), 0, pr_ok
                    else:
                        todo, part, done = ((kv, g_re, sinT, 1.0), (mu, g_im, cosT, -1.0)), 1, pi_ok
                    dve.wait_ge(qr_ok, c + 1)
                    dve.wait_ge(qi_ok, c + 1)
                    for s in range(SEQ):
                        t = slice(s * S, (s + 1) * S)
                        for n, (o, g, w, sign) in enumerate(todo):
                            dve.tensor_tensor_reduce(out=o[:, c, t], in0=g[:, c, t], in1=w[:, c, t], scale=sign,
                                                     scalar=0.0, op0=ALU.mult, op1=ALU.add,
                                                     accum_out=gst[:, c, n, part, s:s + 1]).then_inc(done, 1)
                elif step == "means":
                    dve.wait_ge(gm_ps, c + 1)
                    m = bank("means", c)[:, 0:3 * SEQ].rearrange("p (k s) -> p k s", s=SEQ)
                    dve.tensor_copy(gmean[:, c], m).then_inc(vs, 1)
                    dve.wait_ge(vs, 3 * c + 1)
                    dve.tensor_tensor(gw[:, c, 0:2, :], gmean[:, c, 0:2, :], gmean[:, c, 0:2, :], ALU.mult).then_inc(vs, 1)
                    dve.wait_ge(vs, 3 * c + 2)
                    dve.scalar_tensor_tensor(out=gvar[:, c, :], in0=gmean[:, c, 2, :], scalar=EPS_GROUP,
                                             in1=gw[:, c, 0, :], op0=ALU.add, op1=ALU.subtract).then_inc(vs, 1)
                    dve.wait_ge(vs, 3 * c + 3)
                    dve.tensor_tensor(gvar[:, c, :], gvar[:, c, :], gw[:, c, 1, :], ALU.subtract).then_inc(gm_ok, 1)
                elif step == "gated":
                    dve.wait_ge(gate_ok, c + 1)
                    dve.wait_ge(yn_ok, c + 1)
                    dve.tensor_tensor(y_re[:, c, :], y_re[:, c, :], gate[:, c, :], ALU.mult).then_inc(z_ok, 1)
                elif step in ("mul2", "add2"):
                    ready, done, by, op = ((n2_ok, u2_ok, s2_bc, ALU.mult) if step == "mul2" else
                                           (u2_ok, a2_ok, b2_bc, ALU.add))
                    dve.wait_ge(s_bc, 16 * 3)
                    dve.wait_ge(ready, c + 1)
                    dve.tensor_tensor(a2_tok[:, tl(c), :], a2_tok[:, tl(c), :],
                                      by[:, :].unsqueeze(1).to_broadcast([P, TC, D]), op).then_inc(done, 1)
                elif step == "x2":
                    dve.wait_ge(rs_ok[3], c + 1)
                    for k in range(TC):
                        t = TC * c + k
                        ins = dve.scalar_tensor_tensor(out=x2_tok[:, t, :], in0=a2_tok[:, t, :],
                                                       scalar=rstd[:, 3, t:t + 1], in1=x_tok[:, t, :],
                                                       op0=ALU.mult, op1=ALU.add)
                    ins.then_inc(x2_ok, 1)
                elif step.startswith("route"):
                    n = int(step[5:])
                    R, Q = ro[:, c], r4[:, c]
                    lg = bank("logits", c)[:, 0:TC * E].rearrange("p (t e) -> p t e", e=E)
                    top = R[:, 2]
                    most, second = top[:, :, 0], top[:, :, 1]
                    if n == 0:
                        dve.wait_ge(lg_ps, c + 1)
                        for k in range(TC):
                            ins = dve.max(top[:, k, :], lg[:, k, :])
                    else:
                        dve.wait_ge(rt[n - 1], c + 1)
                    if n == 1:
                        dve.tensor_tensor(R[:, 3], lg, over_e(second), ALU.is_equal)
                        dve.tensor_tensor(R[:, 4], lg, over_e(second), ALU.is_gt)
                        dve.tensor_tensor(Q[:, 0], most, second, ALU.is_equal)
                        ins = dve.tensor_tensor(R[:, 0], lg, over_e(most), ALU.subtract)
                    elif n == 2:
                        ins = dve.tensor_tensor_scan(R[:, 5].rearrange("p t e -> p (t e)"),
                                                     first_e[:, :, :].rearrange("p t e -> p (t e)"),
                                                     R[:, 3].rearrange("p t e -> p (t e)"), 0.0, ALU.mult, ALU.add)
                    elif n == 3:
                        ins = dve.tensor_tensor(R[:, 5], R[:, 5], over_e(Q[:, 0]), ALU.subtract)
                    elif n == 4:
                        ins = dve.scalar_tensor_tensor(out=R[:, 5], in0=R[:, 5], scalar=1.0, in1=R[:, 3],
                                                       op0=ALU.is_le, op1=ALU.mult)
                    elif n == 5:
                        dve.wait_ge(th_ok, c + 1)
                        dve.tensor_tensor(R[:, 6], R[:, 5], R[:, 4], ALU.add)
                        ins = dve.tensor_scalar(R[:, 7], R[:, 1], -1.0, 1.0, ALU.mult, ALU.add)
                    elif n == 6:
                        ins = dve.reciprocal(R[:, 7], R[:, 7])
                    elif n == 7:
                        ins = dve.scalar_tensor_tensor(out=R[:, 8], in0=R[:, 1], scalar=1.0, in1=R[:, 7],
                                                       op0=ALU.add, op1=ALU.mult)
                    elif n == 8:
                        dve.tensor_reduce(out=Q[:, 1], in_=R[:, 8], op=ALU.add, axis=AX.X)
                        ins = dve.tensor_tensor(R[:, 9], R[:, 8], R[:, 6], ALU.mult)
                    elif n == 9:
                        ins = dve.tensor_reduce(out=Q[:, 2], in_=R[:, 9], op=ALU.add, axis=AX.X)
                    elif n == 10:
                        ins = dve.scalar_tensor_tensor(out=Q[:, 3], in0=Q[:, 1], scalar=EPS_MOE, in1=Q[:, 2],
                                                       op0=ALU.mult, op1=ALU.add)
                    elif n == 11:
                        ins = dve.reciprocal(Q[:, 4], Q[:, 3])
                    elif n == 12:
                        ins = dve.tensor_tensor(Q[:, 5], Q[:, 2], Q[:, 4], ALU.mult)
                    elif n == 13:
                        dve.tensor_scalar(Q[:, 6], Q[:, 5], EPS_MOE, None, ALU.max)
                        ins = dve.tensor_scalar(Q[:, 7], Q[:, 5], EPS_MOE, 1.0, ALU.mult, ALU.add)
                    elif n == 14:
                        dve.reciprocal(Q[:, 8], Q[:, 6])
                        ins = dve.tensor_tensor(Q[:, 9], Q[:, 7], Q[:, 4], ALU.mult)
                    elif n == 15:
                        ins = dve.tensor_tensor(Q[:, 10], Q[:, 9], Q[:, 8], ALU.mult)
                    elif n == 16:
                        ins = dve.scalar_tensor_tensor(out=Q[:, 11], in0=Q[:, 10], scalar=1.0 / EPS[5],
                                                       in1=Q[:, 10], op0=ALU.mult, op1=ALU.mult)
                    elif n == 17:
                        ins = dve.reciprocal(epsf[:, tl(c)], Q[:, 11])
                    ins.then_inc(epsf_ok if n == 17 else rt[n], 1)
                elif step.startswith("weigh"):
                    e = int(step[-1])
                    dve.wait_ge(m_ps, c + 1)
                    dve.wait_ge(wb_ps, E * c + e + 1)
                    dve.tensor_tensor(xs[e][:, c, :], bank(f"spread{e}", c), t4T[:, c, :],
                                      ALU.mult).then_inc(xs_ok, 1)
                elif step == "last_sum":
                    dve.wait_ge(rs_ok[5], c + 1)
                    for k in range(TC):
                        t = TC * c + k
                        dve.scalar_tensor_tensor(out=tiles(o_tok[:, c, :])[:, k, :], in0=bank("expert0", c)[:, tok(k)],
                                                 scalar=rstd[:, 5, t:t + 1], in1=x2_tok[:, t, :],
                                                 op0=ALU.mult, op1=ALU.add).then_inc(last_ok, 1)


_INS = ['x', 'Wq', 'Wk', 'Wv', 'Wa', 'Wg', 'Wo', 'gn_scale', 'gn_bias', 'ln1_scale', 'ln1_bias',
        'W1', 'b1', 'W2', 'b2', 'ln2_scale', 'ln2_bias']
_INS = ["L0_attn_" + n for n in _INS] + ["L0_ffn_" + n for n in ('router_w', 'router_b', 'expert_weights')]
_OUTS = [((8, 256, 128), 'float32')]


def kernel(**inputs):
    import numpy as _np
    import concourse.bacc as _bacc
    from concourse import mybir as _mybir
    from concourse.bass_utils import run_bass_kernel_spmd as _run

    nc = _bacc.Bacc("TRN2", target_bir_lowering=False, num_devices=1)
    arrays, args = {}, []
    for name in _INS:
        a = _np.ascontiguousarray(inputs[name])
        arrays[f"in_{name}_dram"] = a
        args.append(nc.dram_tensor(f"in_{name}_dram", a.shape, _mybir.dt.from_np(a.dtype), kind="ExternalInput").ap())
    for i, (shape, dtype) in enumerate(_OUTS):
        dt = _mybir.dt.from_np(_np.dtype(dtype))
        args.append(nc.dram_tensor(f"out_{i}_dram", shape, dt, kind="ExternalOutput").ap())
    sandwich(nc, *args)
    r = _run(nc, [arrays], core_ids=[0])
    got = tuple(r.results[0][f"out_{i}_dram"] for i in range(len(_OUTS)))
    return got[0]
```
